# Optimizing a Trainium2 kernel written in Bass

```python
import numpy as np
import jax
import jax.numpy as jnp

def _softmax(x, axis=-1):
    return jax.nn.softmax(x, axis=axis)

def _gelu(x):
    return jax.nn.gelu(x, approximate=True)

def _silu(x):
    return jax.nn.silu(x)

def _sigmoid(x):
    return jax.nn.sigmoid(x)

def _layernorm(x, axis=-1, eps=1e-05):
    m = jnp.mean(x, axis=axis, keepdims=True)
    v = jnp.var(x, axis=axis, keepdims=True)
    return (x - m) / jnp.sqrt(v + eps)

def _scatter_add(tgt, idx, src, axis=0):
    return tgt.at[idx].add(src)

def _segment_sum(src, seg, n):
    return jax.ops.segment_sum(src, seg, n)
kernel_name = 'mk_vit_tower_d1_tok_img256_r4_9e0397'

def setup_inputs(seed: int=0):
    np.random.seed(seed)
    _w = jnp.asarray

    def _rec_inputs():
        import jax
        import jax.numpy as jnp
        _rk = jax.random.key(seed)
        x = -0.00040386 + 0.999972 * jax.random.normal(jax.random.fold_in(_rk, 1), (64, 128, 64, 3), jnp.float32)
        return x
    x = _rec_inputs()

    def _L0_tok_setup():
        import jax, jax.numpy as jnp
        import numpy as np
        B, T, J, LAT = (128, 128, 64, 64)
        EPS = 1e-05

        def layernorm(x, g, b):
            m = jnp.mean(x, axis=-1, keepdims=True)
            v = jnp.var(x, axis=-1, keepdims=True)
            return (x - m) * jax.lax.rsqrt(v + EPS) * g + b

        def conv2d(x, w, b, pad):
            y = jax.lax.conv_general_dilated(x, w, window_strides=(1, 1), padding=pad, dimension_numbers=('NCHW', 'OIHW', 'NCHW'))
            return y + b[None, :, None, None]
        key = jax.random.key(seed)
        ks = jax.random.split(key, 10)
        s = 0.02
        return {'x': jax.random.normal(ks[0], (B, T, J, 3), dtype=jnp.float32), 'ln0_g': jnp.ones((J * 3,), jnp.float32), 'ln0_b': jnp.zeros((J * 3,), jnp.float32), 'ln1_g': jnp.ones((J * 2,), jnp.float32), 'ln1_b': jnp.zeros((J * 2,), jnp.float32), 'conv1_w': jax.random.normal(ks[1], (T, T, 5, 3), jnp.float32) * s, 'conv1_b': jnp.zeros((T,), jnp.float32), 'conv2_w': jax.random.normal(ks[2], (T, T, 5, 2), jnp.float32) * s, 'conv2_b': jnp.zeros((T,), jnp.float32), 'conv3_w': jax.random.normal(ks[3], (2 * T, T, 5, 2), jnp.float32) * s, 'conv3_b': jnp.zeros((2 * T,), jnp.float32), 'out_w': jax.random.normal(ks[4], (2 * J, LAT), jnp.float32) * s, 'out_b': jnp.zeros((LAT,), jnp.float32)}
    _L0_tok_all = _L0_tok_setup()
    _L0_tok_in = {k: v for k, v in _L0_tok_all.items() if k in ('ln0_g', 'ln0_b', 'ln1_g', 'ln1_b', 'conv1_w', 'conv1_b', 'conv2_w', 'conv2_b', 'conv3_w', 'conv3_b', 'out_w', 'out_b')}
    del _L0_tok_all

    def _L0_attn_setup():
        import jax, jax.numpy as jnp
        import numpy as np
        D_MODEL = 64
        N_HEAD = 8

        def _l1_scores(q, k):
            scale = 1.0 / np.sqrt(q.shape[-1]).astype(np.float32)
            q_sbhw = q.transpose(1, 0, 2, 3)

            def one_query(qs):
                return -jnp.sum(jnp.abs(qs[:, None, :, :] - k), axis=-1) * scale
            s = jax.lax.map(one_query, q_sbhw)
            return s.transpose(1, 0, 2, 3)
        key = jax.random.key(seed)
        ks = jax.random.split(key, 3)
        b, t = (4, 250)
        x = jax.random.normal(ks[0], (b, t, D_MODEL), jnp.float32)
        wqv_w = 0.005 * jax.random.normal(ks[1], (3 * N_HEAD * D_MODEL, D_MODEL), jnp.float32)
        wqv_b = jnp.zeros((3 * N_HEAD * D_MODEL,), jnp.float32)
        wk = 0.005 * jnp.ones((N_HEAD, D_MODEL), jnp.float32)
        fanin_w = 0.005 * jax.random.normal(ks[2], (D_MODEL, D_MODEL), jnp.float32)
        fanin_b = jnp.zeros((D_MODEL,), jnp.float32)
        return dict(x=x, wqv_w=wqv_w, wqv_b=wqv_b, wk=wk, fanin_w=fanin_w, fanin_b=fanin_b)
    _L0_attn_all = _L0_attn_setup()
    _L0_attn_in = {k: v for k, v in _L0_attn_all.items() if k in ('wqv_w', 'wqv_b', 'wk', 'fanin_w', 'fanin_b')}
    del _L0_attn_all

    def _L0_ffn_setup():
        import jax, jax.numpy as jnp
        import numpy as np
        B, K, D = (128, 16, 64)
        E = 32
        H = int(D * 0.25)
        key = jax.random.key(seed)
        ks = jax.random.split(key, 7)
        d_rs = D ** (-0.5)
        h_rs = H ** (-0.5)
        x = jax.random.normal(ks[0], (B, K, D), dtype=jnp.float32)
        router_w = jax.random.uniform(ks[1], (E, D), jnp.float32, -d_rs, d_rs)
        router_b = jax.random.uniform(ks[2], (E,), jnp.float32, -d_rs, d_rs)
        W1 = jax.random.uniform(ks[3], (E, D, H), jnp.float32, -h_rs, h_rs)
        b1 = jax.random.uniform(ks[4], (E, H), jnp.float32, -h_rs, h_rs)
        W2 = jax.random.uniform(ks[5], (E, H, D), jnp.float32, -d_rs, d_rs)
        b2 = jax.random.uniform(ks[6], (E, D), jnp.float32, -d_rs, d_rs)
        return {'x': x, 'router_w': router_w, 'router_b': router_b, 'W1': W1, 'b1': b1, 'W2': W2, 'b2': b2}
    _L0_ffn_all = _L0_ffn_setup()
    _L0_ffn_in = {k: v for k, v in _L0_ffn_all.items() if k in ('router_w', 'router_b', 'W1', 'b1', 'W2', 'b2')}
    del _L0_ffn_all
    return {'x': x, 'L0_tok_ln0_g': _L0_tok_in['ln0_g'], 'L0_tok_ln0_b': _L0_tok_in['ln0_b'], 'L0_tok_ln1_g': _L0_tok_in['ln1_g'], 'L0_tok_ln1_b': _L0_tok_in['ln1_b'], 'L0_tok_conv1_w': _L0_tok_in['conv1_w'], 'L0_tok_conv1_b': _L0_tok_in['conv1_b'], 'L0_tok_conv2_w': _L0_tok_in['conv2_w'], 'L0_tok_conv2_b': _L0_tok_in['conv2_b'], 'L0_tok_conv3_w': _L0_tok_in['conv3_w'], 'L0_tok_conv3_b': _L0_tok_in['conv3_b'], 'L0_tok_out_w': _L0_tok_in['out_w'], 'L0_tok_out_b': _L0_tok_in['out_b'], 'L0_attn_wqv_w': _L0_attn_in['wqv_w'], 'L0_attn_wqv_b': _L0_attn_in['wqv_b'], 'L0_attn_wk': _L0_attn_in['wk'], 'L0_attn_fanin_w': _L0_attn_in['fanin_w'], 'L0_attn_fanin_b': _L0_attn_in['fanin_b'], 'L0_ffn_router_w': _L0_ffn_in['router_w'], 'L0_ffn_router_b': _L0_ffn_in['router_b'], 'L0_ffn_W1': _L0_ffn_in['W1'], 'L0_ffn_b1': _L0_ffn_in['b1'], 'L0_ffn_W2': _L0_ffn_in['W2'], 'L0_ffn_b2': _L0_ffn_in['b2']}

def reference(x, L0_tok_ln0_g, L0_tok_ln0_b, L0_tok_ln1_g, L0_tok_ln1_b, L0_tok_conv1_w, L0_tok_conv1_b, L0_tok_conv2_w, L0_tok_conv2_b, L0_tok_conv3_w, L0_tok_conv3_b, L0_tok_out_w, L0_tok_out_b, L0_attn_wqv_w, L0_attn_wqv_b, L0_attn_wk, L0_attn_fanin_w, L0_attn_fanin_b, L0_ffn_router_w, L0_ffn_router_b, L0_ffn_W1, L0_ffn_b1, L0_ffn_W2, L0_ffn_b2):
    import jax
    import jax.numpy as jnp

    def _L0_tok_ref(x, ln0_g, ln0_b, ln1_g, ln1_b, conv1_w, conv1_b, conv2_w, conv2_b, conv3_w, conv3_b, out_w, out_b):
        import jax, jax.numpy as jnp
        import numpy as np
        B, T, J, LAT = (128, 128, 64, 64)
        EPS = 1e-05

        def layernorm(x, g, b):
            m = jnp.mean(x, axis=-1, keepdims=True)
            v = jnp.var(x, axis=-1, keepdims=True)
            return (x - m) * jax.lax.rsqrt(v + EPS) * g + b

        def conv2d(x, w, b, pad):
            y = jax.lax.conv_general_dilated(x, w, window_strides=(1, 1), padding=pad, dimension_numbers=('NCHW', 'OIHW', 'NCHW'))
            return y + b[None, :, None, None]
        b, t, j, d = x.shape
        h = layernorm(x.reshape(b, t, j * 3), ln0_g, ln0_b).reshape(b, t, j, 3)
        h = jax.nn.relu(conv2d(h, conv1_w, conv1_b, ((2, 2), (1, 1))))
        h = layernorm(h.reshape(b, t, j * 3), ln0_g, ln0_b).reshape(b, t, j, 3)
        h = jax.nn.relu(conv2d(h, conv2_w, conv2_b, ((2, 2), (0, 0))))
        h = layernorm(h.reshape(b, t, j * 2), ln1_g, ln1_b).reshape(b, t, j, 2)
        h = jax.nn.relu(conv2d(h, conv3_w, conv3_b, ((2, 2), (0, 0))))
        h = h.reshape(b, 2 * t, j)
        res = jnp.concatenate([h[:, :t, :], h[:, t:, :]], axis=2)
        res = layernorm(res, ln1_g, ln1_b)
        return res @ out_w + out_b

    def _L0_attn_ref(x, wqv_w, wqv_b, wk, fanin_w, fanin_b):
        import jax, jax.numpy as jnp
        import numpy as np
        D_MODEL = 64
        N_HEAD = 8

        def _l1_scores(q, k):
            scale = 1.0 / np.sqrt(q.shape[-1]).astype(np.float32)
            q_sbhw = q.transpose(1, 0, 2, 3)

            def one_query(qs):
                return -jnp.sum(jnp.abs(qs[:, None, :, :] - k), axis=-1) * scale
            s = jax.lax.map(one_query, q_sbhw)
            return s.transpose(1, 0, 2, 3)
        b, t, d = x.shape
        h = N_HEAD
        v = (x @ wqv_w.T + wqv_b).reshape(b, t, 3 * h, d)
        q, vf, vb = (v[:, :, :h], v[:, :, h:2 * h], v[:, :, 2 * h:])
        k = x[:, :, None, :] * wk[None, None]
        a = _l1_scores(q, k)
        a = jnp.concatenate([a, jnp.zeros((b, 1, t, h), a.dtype)], axis=1)
        a = jax.nn.softmax(a, axis=1)[:, :t]
        bf = jnp.einsum('bsdh,bshw->bdhw', a, vf)
        bb = jnp.einsum('bdsh,bshw->bdhw', a, vb)
        o = (bf + bb).sum(axis=2).reshape(b, t, d)
        y = o * jax.nn.sigmoid(1.702 * o)
        y = y @ fanin_w.T + fanin_b
        return x + y

    def _L0_ffn_ref(x, router_w, router_b, W1, b1, W2, b2):
        import jax, jax.numpy as jnp
        import numpy as np
        B, K, D = (128, 16, 64)
        E = 32
        H = int(D * 0.25)
        xf = x.reshape(-1, D)
        logits = xf @ router_w.T + router_b
        idx = jnp.argmax(logits, axis=-1)
        w1t = jnp.take(W1, idx, axis=0)
        h = jnp.einsum('nd,ndh->nh', xf, w1t) + jnp.take(b1, idx, axis=0)
        h = jax.nn.relu(h)
        w2t = jnp.take(W2, idx, axis=0)
        out = jnp.einsum('nh,nhd->nd', h, w2t) + jnp.take(b2, idx, axis=0)
        out = jax.nn.relu(out)
        return out.reshape(x.shape)
    h = _L0_tok_ref(x, L0_tok_ln0_g, L0_tok_ln0_b, L0_tok_ln1_g, L0_tok_ln1_b, L0_tok_conv1_w, L0_tok_conv1_b, L0_tok_conv2_w, L0_tok_conv2_b, L0_tok_conv3_w, L0_tok_conv3_b, L0_tok_out_w, L0_tok_out_b)
    h = h + _L0_attn_ref(_layernorm(h, axis=-1), L0_attn_wqv_w, L0_attn_wqv_b, L0_attn_wk, L0_attn_fanin_w, L0_attn_fanin_b)
    h = h + _L0_ffn_ref(_layernorm(h, axis=-1), L0_ffn_router_w, L0_ffn_router_b, L0_ffn_W1, L0_ffn_b1, L0_ffn_W2, L0_ffn_b2)
    return h

_drawn_inputs = setup_inputs


def setup_inputs(seed=0):
    import zlib

    import numpy as np

    out = dict(_drawn_inputs(seed))
    spreads = {'L0_tok_ln0_g': (1.0, 0.2),
     'L0_tok_ln0_b': (0.0, 0.1),
     'L0_tok_ln1_g': (1.0, 0.2),
     'L0_tok_ln1_b': (0.0, 0.1),
     'L0_tok_conv1_b': (0.0, 0.1),
     'L0_tok_conv2_b': (0.0, 0.1),
     'L0_tok_conv3_b': (0.0, 0.1),
     'L0_tok_out_b': (0.0, 0.1),
     'L0_attn_wqv_b': (0.0, 0.685),
     'L0_attn_wk': (0.004999999888241291, 0.6),
     'L0_attn_fanin_b': (0.0, 0.1)}
    factors = {'L0_attn_wqv_w': 8.0, 'L0_attn_fanin_w': 5.469, 'L0_ffn_b1': 4.026}
    for name, (base, spread) in spreads.items():
        noise = np.random.default_rng([zlib.crc32(name.encode()), seed]).standard_normal(out[name].shape)
        drawn = base * np.exp(spread * noise) if base else spread * noise
        out[name] = jnp.asarray(drawn.astype(out[name].dtype))
    for name, factor in factors.items():
        out[name] = (out[name] * factor).astype(out[name].dtype)
    return out
```

```python
from contextlib import ExitStack

import concourse.bass as bass
from concourse import mybir

F32 = mybir.dt.float32
BF16 = mybir.dt.bfloat16
ALU = mybir.AluOpType
ACT = mybir.ActivationFunctionType
AX = mybir.AxisListType

T = 128
J = 64
LAT = 64
HEADS = 8
HW = HEADS * LAT
E, HID = 32, 16
EPS = 1e-5
SB = 16
CHUNKS = T // SB
RING = 4
SLOTS = 2 * CHUNKS * HEADS
NOT_CHOSEN = -1e30

SHARED = [(2, 5), (1, 5), (2, 5), (1, 5), (2, 5), (1, 5), (2, 5), (0, 2, 4, 6)]
assert len(SHARED) == CHUNKS
A_BATCH = sum(len(x) for x in SHARED)
A_PAIR = 2 * A_BATCH
D_PAIR = SLOTS - A_PAIR
LEVELS = 6


def shared(slot):
    c, h = slot // HEADS % CHUNKS, slot % HEADS
    return h in SHARED[c]


D_BEFORE = [sum(not shared(x) for x in range(s)) for s in range(SLOTS + 1)]
A_BEFORE = [sum(shared(x) for x in range(s)) for s in range(SLOTS + 1)]


class Steps:

    def __init__(self, names):
        self.names = names.split()

    def after(self, n, name):
        return n * len(self.names) + (self.names.index(name) + 1)


TOK_PE = Steps("conv1 conv2 conv3 turn out")
TOK_ACT = Steps("relu1 relu2 relu3a relu3b turned")
LN = "stat{0}0 stat{0}1 wait{0} aggr{0}0 aggr{0}1 eps{0} "
LN_APPLY = "gain{0}0 gain{0}1 shift{0}0 shift{0}1 "
TOK_DVE = Steps("".join(LN.format(x) + LN_APPLY.format(x) for x in "abc") + LN.format("d") + "norm0 norm1 h")
TOK_POOL = Steps("rstda rstdb rstdc rstdd")
NORM_DVE = Steps("stat0 stat1 wait aggr0 aggr1 eps x0 x1")
NORM_POOL = Steps("rstd hx")
NORM_PE = Steps("turn")
NORM_ACT = Steps("turned0 turned")
HAND_ACT = Steps("xT hx")
KQ_POOL = Steps("k rest1 part3 qpart3")
KQ_ACT = Steps("part1 part2 kTa kTb qpart1 qpart2")
KQ_PE = Steps("kTa kTb q")
KQ_DVE = Steps("qrest1")
AT_PE = Steps("vf vb turna turnb pv")
AT_ACT = Steps("vf vb exp0 exp1 exp2 exp3 exp4 exp5 exp6 exp7 turneda turnedb gexp")
AT_DVE = Steps("den rden gate1 gate2 gate")
AT_POOL = Steps("scalea scaleb")
EX_PE = Steps("fan turn route turnoh hida hidb out back")
EX_DVE = Steps("h2 stat0 stat1 wait aggr0 aggr1 eps x0 x1 max eq rev max2 noh result")
EX_POOL = Steps("rstd")
EX_ACT = Steps("turned0 turned noh oh relua relub relu0 relu")

KQ_AT = dict(k=0, part1=1, rest1=2, part2=3, part3=4, kTa=8, kTb=10, q=12)
AT_AT = dict(vf=2, vb=4, exp=8, den=17, scalea=18, scaleb=20, turna=22, turnb=25, pv=28, gexp=36)
SECOND = 66
EX_AT = dict(fan=39, h2=40, rstd=43, x=45, turn=47, route=50, pick=51, turnoh=53, hida=56, hidb=58, out=61, back=64)
NORM_AT = dict(stat=36, rstd=38, x=40, turn=42, hx=45)
HAND_AT = dict(xT=38, hx=44)
TOK_AT = dict(a=5, conv1=12, b=29, conv2=36, c=48, conv3=55, d=77, turn=83, out=87)


def vit_tower(nc, a, out):
    PAIRS = a["x"].shape[0] // 2
    x_v = a["x"].rearrange("b t f -> t b f")
    out_v = out.rearrange("b t w -> t b w")

    with ExitStack() as ctx:
        def sb(name, shape, dt=F32):
            return ctx.enter_context(nc.sbuf_tensor(name, shape, dt))

        def sem(name):
            return ctx.enter_context(nc.semaphore(name))

        ident = sb("ident", [T, T])
        ident_b = sb("ident_b", [T, T], BF16)
        ln0g = sb("ln0g", [T, 3 * J])
        ln0b = sb("ln0b", [T, 3 * J])
        ln1g = sb("ln1g", [T, 2 * J])
        ln1b = sb("ln1b", [T, 2 * J])
        ln1g_col = sb("ln1g_col", [T, 1])
        ln1b_col = sb("ln1b_col", [T, 1])
        w1 = sb("w1", [T, 15, T])
        w2 = sb("w2", [T, 10, T])
        w3 = sb("w3", [T, 10, 2 * T])
        b1 = sb("b1", [T, 1])
        b2 = sb("b2", [T, 1])
        b3 = sb("b3", [T, 2])
        wout = sb("wout", [T, LAT])
        bout = sb("bout", [T, 2, LAT])
        wqv = sb("wqv", [T, 3 * HW])
        wk = sb("wk", [T, HEADS, LAT])
        wfan = sb("wfan", [T, LAT])
        wroute = sb("wroute", [T, E])
        we1 = sb("we1", [T, E * HID])
        we2 = sb("we2", [T, 4, LAT])
        be2 = sb("be2", [T, LAT])
        rank = sb("rank", [T, 2, E])
        half = sb("half", [T, 2])
        one = sb("one", [T, 1])
        spare = sb("spare", [T, 1])

        xin = sb("xin", [T, 2, 3 * J])
        lt = sb("lt", [T, 2, 3 * J])
        c1in = sb("c1in", [T, 2, J + 4, 3])
        c2in = sb("c2in", [T, 2, J + 4, 3])
        c3in = sb("c3in", [T, 2, J + 4, 2])
        y1 = sb("y1", [T, 2, 3 * J])
        y2 = sb("y2", [T, 2, 2 * J])
        res = sb("res", [T, 2, 2 * J])
        resn = sb("resn", [T, 2, 2 * J])
        resT = sb("resT", [T, 2, T])
        st = {k: sb("st" + k, [T, 2, 6]) for k in "abcdne"}
        mv = {k: sb("mv" + k, [T, 2, 2]) for k in "abcdne"}
        ve = {k: sb("ve" + k, [T, 2]) for k in "abcdne"}
        rstd = {k: sb("rstd" + k, [T, 2]) for k in "abcdne"}
        h = sb("h", [T, 2, LAT])
        x1 = sb("x1", [T, 2, LAT])
        x1T = sb("x1T", [T, 2 * T])
        x1T_late = sb("x1T_late", [T, 2 * T])
        hx = sb("hx", [T, 2, LAT])
        hx_late = sb("hx_late", [T, 2, LAT])
        k = sb("k", [T, HEADS, 2, 32])
        kparts = sb("kparts", [T, HEADS, 2, 3, 32], BF16)
        kT = sb("kT", [T, 2, HEADS, 2, T], BF16)
        qrest = sb("qrest", [T, HW])
        qparts = sb("qparts", [T, 2, 3, HW], BF16)
        flat = sb("flat", [T, RING, SB, HW], BF16)
        absd = sb("absd", [T, 2, 2, 2, SB, 32])
        S = sb("S", [T, 2, HEADS, T])
        P = sb("P", [T, HEADS, T])
        PT = sb("PT", [T, HEADS, T])
        den = sb("den", [T, HEADS])
        den1 = sb("den1", [T, HEADS])
        rden = sb("rden", [T, HEADS])
        v = sb("v", [T, 2, HW])
        g1 = sb("g1", [T, T])
        g2 = sb("g2", [T, T])
        g3 = sb("g3", [T, T])
        gT = sb("gT", [T, 2, T])
        h2 = sb("h2", [T, 2, LAT])
        x2 = sb("x2", [T, 2, LAT])
        xa = sb("xa", [T, 2 * T])
        top = sb("top", [T, 2])
        eq = sb("eq", [T, 2, E])
        rev = sb("rev", [T, 2, E])
        top2 = sb("top2", [T, 2])
        noh = sb("noh", [T, 2, E])
        ohT = sb("ohT", [T, 2 * T])
        hT = sb("hT", [T, 4, 2 * T])
        fT = sb("fT", [T, T])
        result = sb("result", [T, 2, LAT])

        psD = ctx.enter_context(nc.psum_tensor("psD", [T, 2, 2, SB, 32], F32))
        psA = ctx.enter_context(nc.psum_tensor("psA", [T, 2, SB, 32], F32))
        psC = ctx.enter_context(nc.psum_tensor("psC", [T, 512], F32))
        psZ = ctx.enter_context(nc.psum_tensor("psZ", [T, 512], F32))
        psZb = psZ[:, :].bitcast(BF16)

        loaded = sem("loaded")
        ready = sem("ready")
        zeroed = sem("zeroed")
        x_in = sem("x_in")
        stored = sem("stored")
        flat_in = [sem(f"flat_in{n}") for n in range(RING)]
        d_made = sem("d_made")
        d_done = sem("d_done")
        a_made = sem("a_made")
        a_abs = sem("a_abs")
        a_tree = sem("a_tree")
        tok_pe, tok_act, tok_dve, tok_pool = (sem("tok_" + e) for e in ("pe", "act", "dve", "pool"))
        norm_pe, norm_act, norm_dve, norm_pool = (sem("norm_" + e) for e in ("pe", "act", "dve", "pool"))
        hand_act = sem("hand_act")
        kq_pe, kq_act, kq_dve, kq_pool = (sem("kq_" + e) for e in ("pe", "act", "dve", "pool"))
        at_pe, at_act, at_dve, at_pool = (sem("at_" + e) for e in ("pe", "act", "dve", "pool"))
        ex_pe, ex_act, ex_dve, ex_pool = (sem("ex_" + e) for e in ("pe", "act", "dve", "pool"))

        weights = [
            (ident, a["ident"]), (ln0g, a["ln0g"]), (ln0b, a["ln0b"]), (w1, a["w1"]), (b1, a["b1"]),
            (w2, a["w2"]), (b2, a["b2"]), (ln1g, a["ln1g"]), (ln1b, a["ln1b"]), (w3, a["w3"]), (b3, a["b3"]),
            (ln1g_col, a["ln1g_col"]), (ln1b_col, a["ln1b_col"]), (wout, a["wout"]), (bout, a["bout"]),
            (wk, a["wk"]), (rank, a["rank"]), (we2, a["we2"]),
        ]
        parts_of = [
            (wqv[0:65, :], a["wqv"]), (wfan[0:65, :], a["wfan"]), (wroute[0:65, :], a["wroute"]),
            (we1[0:65, :], a["we1"]), (we1[96:128, :], a["shut"]), (be2[0:E, :], a["be2"]),
        ]
        READY = 18
        LOADED = 16 * (len(weights) + len(parts_of))
        block = ctx.enter_context(nc.Block())

        def program(eng, prologue, iteration, epilogue):
            prologue()
            iteration(0, late=False)
            with eng.Fori(1, PAIRS - 2) as i:
                iteration(i)
            iteration(PAIRS - 2, tokens=False)
            iteration(PAIRS - 1, tokens=False, ahead=False)
            epilogue()

        @block.sync
        def _(sp):
            sp.dma_start(xin[:, :, :], x_v[:, 0:2, :]).then_inc(x_in, 16)
            for dst, src in weights:
                sp.dma_start(dst[:], src).then_inc(loaded, 16)
            sp.wait_ge(zeroed, 1)
            for dst, src in parts_of:
                sp.dma_start(dst, src).then_inc(loaded, 16)

            def load_x(p):
                sp.wait_ge(tok_dve, TOK_DVE.after(p - 1, "gaina1"))
                sp.dma_start(xin[:, :, :], x_v[:, bass.ds(2 * p, 2), :]).then_inc(x_in, 16)

            def load_flat(batch, b, c):
                sp.wait_ge(kq_pool, KQ_POOL.after(batch, "qpart3"))
                for part in range(3):
                    sp.dma_start(flat[96 + part:97 + part, c % RING, :, :],
                                 qparts[SB * c:SB * c + SB, b, part, :]).then_inc(flat_in[c % RING], 16)

            def store(p):
                sp.wait_ge(ex_dve, EX_DVE.after(p, "result"))
                sp.dma_start(out_v[:, bass.ds(2 * p, 2), :], result[:, :, :]).then_inc(stored, 16)

            def prologue():
                load_x(1)
                for c in range(RING):
                    load_flat(0, 0, c)

            def iteration(i, late=True, tokens=True, ahead=True):
                if tokens:
                    load_x(i + 2)
                for j in range(2 * CHUNKS):
                    c = j + RING
                    if c < 2 * CHUNKS or ahead:
                        sp.wait_ge(d_made, D_PAIR * i + D_BEFORE[HEADS * (j + 1)])
                        load_flat(2 * i + c // CHUNKS, c // CHUNKS % 2, c % CHUNKS)
                    if j == 8 and late:
                        store(i - 1)

            def epilogue():
                store(PAIRS - 1)
                sp.wait_ge(stored, 16 * PAIRS)

            program(sp, prologue, iteration, epilogue)

        @block.tensor
        def _(pe):
            bank = [None]

            def take_bank(reader, value):
                if bank[0] is not None:
                    pe.wait_ge(*bank[0])
                bank[0] = (reader, value)

            def unit(i, slot):
                b, c, hd = slot // 64, slot // HEADS % CHUNKS, slot % HEADS
                if slot % 64 == 0:
                    pe.wait_ge(kq_act, KQ_ACT.after(2 * i + b, "kTb"))
                if hd == 0:
                    pe.wait_ge(flat_in[c % RING], 48 * (4 * i + (slot // HEADS) // RING + 1))
                if shared(slot):
                    n = A_BEFORE[slot]
                    if not (isinstance(i, int) and i == 0 and n < 1):
                        pe.wait_ge(a_abs, A_PAIR * i + n)
                    dst, made = psA, a_made
                else:
                    n = D_BEFORE[slot]
                    if not (isinstance(i, int) and i == 0 and n < 2):
                        pe.wait_ge(d_done, D_PAIR * i + n - 1)
                    dst, made = psD[:, n % 2], d_made
                for hf in range(2):
                    lo = hd * LAT + hf * 32
                    mm = nc.tensor.matmul(dst[:, hf], kT[0:99, b, hd, hf, :],
                                          flat[0:99, c % RING, :, lo:lo + 32], start=True, stop=True)
                mm.then_inc(made, 1)

            def tok(p, slot):
                n = slot - TOK_AT["conv1"]
                if 0 <= n < 15:
                    dy, m = n // 3, n % 3
                    dx, o, w0, wn = ((1, 0, 0, 3), (0, 1, 0, 2), (2, 0, 1, 2))[m]
                    if n == 0:
                        pe.wait_ge(tok_dve, TOK_DVE.after(p, "shifta1"))
                        if not (isinstance(p, int) and p == 0):
                            pe.wait_ge(tok_dve, TOK_DVE.after(p - 1, "h"))
                    o_v = psC[:, 0:6 * J].rearrange("p (b j w) -> p b j w", b=2, w=3)
                    mm = nc.tensor.matmul(o_v[:, :, :, o:o + wn], w1[:, 3 * dy + dx, :],
                                          c1in[:, :, dy:dy + J, w0:w0 + wn], start=(n == 0), stop=(n == 14))
                    if n == 14:
                        mm.then_inc(tok_pe, 1)
                n = slot - TOK_AT["conv2"]
                if 0 <= n < 10:
                    if n == 0:
                        pe.wait_ge(tok_act, TOK_ACT.after(p, "relu1"))
                        pe.wait_ge(tok_dve, TOK_DVE.after(p, "shiftb1"))
                    dy, dx = n // 2, n % 2
                    mm = nc.tensor.matmul(psC[:, 0:4 * J].rearrange("p (b j w) -> p b j w", b=2, w=2),
                                          w2[:, n, :], c2in[:, :, dy:dy + J, dx:dx + 2],
                                          start=(n == 0), stop=(n == 9))
                    if n == 9:
                        mm.then_inc(tok_pe, 1)
                n = slot - TOK_AT["conv3"]
                if 0 <= n < 20:
                    if n == 0:
                        pe.wait_ge(tok_act, TOK_ACT.after(p, "relu2"))
                        pe.wait_ge(tok_dve, TOK_DVE.after(p, "shiftc1"))
                    hf, m = n // 10, n % 10
                    dy, dx = m // 2, m % 2
                    mm = nc.tensor.matmul(psC[:, hf * T:hf * T + T].rearrange("p (b j) -> p b j", b=2),
                                          w3[:, m, hf * T:hf * T + T], c3in[:, :, dy:dy + J, dx],
                                          start=(m == 0), stop=(m == 9))
                    if n == 19:
                        mm.then_inc(tok_pe, 1)
                if slot == TOK_AT["turn"]:
                    pe.wait_ge(tok_act, TOK_ACT.after(p, "relu3b"))
                    pe.wait_ge(tok_dve, TOK_DVE.after(p, "norm1"))
                    for b in range(2):
                        mm = nc.tensor.transpose(psC[:, b * T:b * T + T], resn[:, b, :], ident[:, :])
                    mm.then_inc(tok_pe, 1)
                if slot == TOK_AT["out"]:
                    pe.wait_ge(tok_act, TOK_ACT.after(p, "turned"))
                    for b in range(2):
                        mm = nc.tensor.matmul(psC[:, b * LAT:b * LAT + LAT], resT[:, b, :], wout[:, :],
                                              start=True, stop=True)
                    mm.then_inc(tok_pe, 1)

            def norm(p, slot):
                if slot == NORM_AT["turn"]:
                    take_bank(norm_act, NORM_ACT.after(p, "turned"))
                    pe.wait_ge(norm_dve, NORM_DVE.after(p, "x1"))
                    nc.tensor.transpose(psZ[:, 0:T], x1[:, :, :].rearrange("p b w -> p (b w)"),
                                        ident[:, :]).then_inc(norm_pe, 1)

            def kq(p, b, slot):
                g = 2 * p + b
                for n, name in enumerate(("kTa", "kTb")):
                    if slot == KQ_AT[name]:
                        take_bank(kq_act, KQ_ACT.after(g, name))
                        pe.wait_ge(kq_pool, KQ_POOL.after(g, "part3"))
                        for m in range(8):
                            mm = nc.tensor.transpose(
                                psZb[0:96, m * T:m * T + T],
                                kparts[:, 4 * n + m // 2, m % 2, :, :].rearrange("p a w -> p (a w)"), ident_b[:, :])
                        mm.then_inc(kq_pe, 1)
                if slot == KQ_AT["q"]:
                    take_bank(kq_dve, KQ_DVE.after(g, "qrest1"))
                    pe.wait_ge(norm_act, NORM_ACT.after(p, "turned"))
                    nc.tensor.matmul(psZ[:, :], x1T[0:65, b * T:b * T + T], wqv[0:65, 0:HW],
                                     start=True, stop=True).then_inc(kq_pe, 1)

            def attend(p, b, slot):
                g = 2 * p + b
                for n, name in enumerate(("vf", "vb")):
                    if slot == AT_AT[name]:
                        take_bank(at_act, AT_ACT.after(g, name))
                        pe.wait_ge(hand_act, HAND_ACT.after(p, "xT"))
                        nc.tensor.matmul(psZ[:, :], x1T_late[0:65, b * T:b * T + T],
                                         wqv[0:65, (1 + n) * HW:(2 + n) * HW],
                                         start=True, stop=True).then_inc(at_pe, 1)
                for n, name in enumerate(("turna", "turnb")):
                    if slot == AT_AT[name]:
                        take_bank(at_act, AT_ACT.after(g, ("turneda", "turnedb")[n]))
                        pe.wait_ge(at_pool, AT_POOL.after(g, ("scalea", "scaleb")[n]))
                        for m in range(4):
                            mm = nc.tensor.transpose(psZ[:, m * T:m * T + T], P[:, 4 * n + m, :], ident[:, :])
                        mm.then_inc(at_pe, 1)
                n = slot - AT_AT["pv"]
                if 0 <= n < HEADS:
                    if n == 0:
                        take_bank(at_dve, AT_DVE.after(g, "gate"))
                        pe.wait_ge(at_act, AT_ACT.after(g, "turnedb"))
                    nc.tensor.matmul(psZ[0:LAT, 0:T], v[:, 1, n * LAT:n * LAT + LAT], P[:, n, :],
                                     start=(n == 0), stop=False)
                    mm = nc.tensor.matmul(psZ[0:LAT, 0:T], v[:, 0, n * LAT:n * LAT + LAT], PT[:, n, :],
                                          start=False, stop=(n == HEADS - 1))
                    if n == HEADS - 1:
                        mm.then_inc(at_pe, 1)

            def experts(p, slot):
                if slot == EX_AT["fan"]:
                    take_bank(ex_dve, EX_DVE.after(p, "h2"))
                    pe.wait_ge(at_dve, AT_DVE.after(2 * p + 1, "gate"))
                    for b in range(2):
                        mm = nc.tensor.matmul(psZ[:, b * LAT:b * LAT + LAT], gT[0:65, b, :], wfan[0:65, :],
                                              start=True, stop=True)
                    mm.then_inc(ex_pe, 1)
                if slot == EX_AT["turn"]:
                    take_bank(ex_act, EX_ACT.after(p, "turned"))
                    pe.wait_ge(ex_dve, EX_DVE.after(p, "x1"))
                    nc.tensor.transpose(psZ[:, 0:T], x2[:, :, :].rearrange("p b w -> p (b w)"),
                                        ident[:, :]).then_inc(ex_pe, 1)
                if slot == EX_AT["route"]:
                    take_bank(ex_dve, EX_DVE.after(p, "eq"))
                    for b in range(2):
                        mm = nc.tensor.matmul(psZ[:, b * E:b * E + E], xa[0:65, b * T:b * T + T], wroute[0:65, :],
                                              start=True, stop=True)
                    mm.then_inc(ex_pe, 1)
                if slot == EX_AT["turnoh"]:
                    take_bank(ex_act, EX_ACT.after(p, "oh"))
                    pe.wait_ge(ex_dve, EX_DVE.after(p, "noh"))
                    for b in range(2):
                        mm = nc.tensor.transpose(psZ[0:E, b * T:b * T + T], noh[:, b, :], ident[:, :])
                    mm.then_inc(ex_pe, 1)
                for n, name in enumerate(("hida", "hidb")):
                    if slot == EX_AT[name]:
                        take_bank(ex_act, EX_ACT.after(p, ("relua", "relub")[n]))
                        for m in range(2):
                            q = 2 * n + m
                            mm = nc.tensor.matmul(psZ[:, m * 256:m * 256 + 256], we1[:, q * T:q * T + T], xa[:, :],
                                                  start=True, stop=True)
                        mm.then_inc(ex_pe, 1)
                if slot == EX_AT["out"]:
                    take_bank(ex_act, EX_ACT.after(p, "relu"))
                    for q in range(4):
                        nc.tensor.matmul(psZ[0:LAT, 0:256], we2[:, q, :], hT[:, q, :], start=(q == 0), stop=False)
                    nc.tensor.matmul(psZ[0:LAT, 0:256], be2[:, :], ohT[:, :], start=False,
                                     stop=True).then_inc(ex_pe, 1)
                if slot == EX_AT["back"]:
                    take_bank(ex_dve, EX_DVE.after(p, "result"))
                    nc.tensor.transpose(psZ[:, 0:2 * LAT], fT[:, :], ident[:, :]).then_inc(ex_pe, 1)

            def prologue():
                pe.wait_ge(loaded, LOADED)
                pe.wait_ge(ready, READY)
                for s in range(SLOTS):
                    tok(0, s)
                for s in range(SLOTS):
                    norm(0, s)
                for s in range(SLOTS):
                    kq(0, 0, s)
                for s in range(SLOTS):
                    tok(1, s)

            def iteration(i, late=True, tokens=True, ahead=True):
                if not isinstance(i, int) or i > 0:
                    bank[0] = (at_dve, AT_DVE.after(2 * i - 2, "gate"))
                for s in range(SLOTS):
                    unit(i, s)
                    if late:
                        attend(i - 1, 1, s)
                    kq(i, 1, s)
                    if late:
                        experts(i - 1, s)
                    if ahead:
                        norm(i + 1, s)
                    attend(i, 0, s - SECOND)
                    if ahead:
                        kq(i + 1, 0, s - SECOND)
                    if tokens:
                        tok(i + 2, s)

            def epilogue():
                for s in range(SLOTS):
                    attend(PAIRS - 1, 1, s)
                    experts(PAIRS - 1, s)

            program(pe, prologue, iteration, epilogue)

        @block.scalar
        def _(act):
            def unit(i, slot):
                if not shared(slot):
                    return
                n = A_BEFORE[slot]
                act.wait_ge(a_made, A_PAIR * i + n + 1)
                if n % 2 == 0 and not (isinstance(i, int) and i == 0 and n < 4):
                    act.wait_ge(a_tree, LEVELS * (A_BATCH * i + n // 2 - 1))
                nc.scalar.activation(absd[:, n // 2 % 2, n % 2], psA[:, :, :, :], ACT.Abs).then_inc(a_abs, 1)

            def tok(p, slot):
                if slot == TOK_AT["conv1"] + 15:
                    act.wait_ge(tok_pe, TOK_PE.after(p, "conv1"))
                    nc.scalar.activation(y1[:, :, :], psC[:, 0:6 * J].rearrange("p (b f) -> p b f", b=2), ACT.Relu,
                                         bias=b1[:, 0:1]).then_inc(tok_act, 1)
                if slot == TOK_AT["conv2"] + 10:
                    act.wait_ge(tok_pe, TOK_PE.after(p, "conv2"))
                    nc.scalar.activation(y2[:, :, :], psC[:, 0:4 * J].rearrange("p (b f) -> p b f", b=2), ACT.Relu,
                                         bias=b2[:, 0:1]).then_inc(tok_act, 1)
                if slot == TOK_AT["conv3"] + 20:
                    act.wait_ge(tok_pe, TOK_PE.after(p, "conv3"))
                    for hf in range(2):
                        nc.scalar.activation(res[:, :, hf * J:hf * J + J],
                                             psC[:, hf * T:hf * T + T].rearrange("p (b j) -> p b j", b=2), ACT.Relu,
                                             bias=b3[:, hf:hf + 1]).then_inc(tok_act, 1)
                if slot == TOK_AT["turn"] + 1:
                    act.wait_ge(tok_pe, TOK_PE.after(p, "turn"))
                    nc.scalar.activation(resT[:, :, :], psC[:, 0:2 * T].rearrange("p (b t) -> p b t", b=2),
                                         ACT.Identity, bias=ln1b_col[:, 0:1], scale=ln1g_col[:, 0:1])\
                        .then_inc(tok_act, 1)

            def norm(p, slot):
                if slot == NORM_AT["turn"] + 1:
                    act.wait_ge(norm_pe, NORM_PE.after(p, "turn"))
                    if not (isinstance(p, int) and p == 0):
                        act.wait_ge(hand_act, HAND_ACT.after(p - 1, "xT"))
                    for b in range(2):
                        nc.scalar.activation(x1T[0:LAT, b * T:b * T + T], psZ[b * LAT:b * LAT + LAT, 0:T],
                                             ACT.Copy).then_inc(norm_act, 1)

            def hand(p, slot):
                if slot == HAND_AT["xT"]:
                    if not (isinstance(p, int) and p == 0):
                        act.wait_ge(at_pe, AT_PE.after(2 * p - 1, "vb"))
                    act.wait_ge(norm_act, NORM_ACT.after(p, "turned"))
                    nc.scalar.activation(x1T_late[0:LAT, :], x1T[0:LAT, :], ACT.Copy).then_inc(hand_act, 1)
                if slot == HAND_AT["hx"]:
                    if not (isinstance(p, int) and p == 0):
                        act.wait_ge(ex_dve, EX_DVE.after(p - 1, "h2"))
                    act.wait_ge(norm_pool, NORM_POOL.after(p, "hx"))
                    nc.scalar.activation(hx_late[:, :, :], hx[:, :, :], ACT.Copy).then_inc(hand_act, 1)

            def kq(p, b, slot):
                g = 2 * p + b
                if slot == KQ_AT["part1"]:
                    act.wait_ge(kq_pool, KQ_POOL.after(g, "k"))
                    nc.scalar.activation(kparts[:, :, :, 0, :], k[:, :, :, :], ACT.Copy).then_inc(kq_act, 1)
                if slot == KQ_AT["part2"]:
                    act.wait_ge(kq_pool, KQ_POOL.after(g, "rest1"))
                    nc.scalar.activation(kparts[:, :, :, 1, :], k[:, :, :, :], ACT.Copy).then_inc(kq_act, 1)
                for n, name in enumerate(("kTa", "kTb")):
                    if slot == KQ_AT[name] + 1:
                        act.wait_ge(kq_pe, KQ_PE.after(g, name))
                        if not (isinstance(p, int) and p == 0):
                            act.wait_ge(d_made, D_PAIR * (p - 1) + D_BEFORE[64 * (b + 1)])
                        nc.scalar.activation(kT[0:96, b, 4 * n:4 * n + 4, :, :].rearrange("p h a t -> p (h a t)"),
                                             psZb[0:96, 0:8 * T], ACT.Copy).then_inc(kq_act, 1)
                if slot == KQ_AT["q"] + 1:
                    act.wait_ge(kq_pe, KQ_PE.after(g, "q"))
                    if not (isinstance(p, int) and p == 0):
                        act.wait_ge(flat_in[RING - 1], 48 * (4 * (p - 1) + 2 * b + 2))
                        act.wait_ge(flat_in[RING - 2], 48 * (4 * (p - 1) + 2 * b + 2))
                        act.wait_ge(flat_in[RING - 3], 48 * (4 * (p - 1) + 2 * b + 2))
                        act.wait_ge(flat_in[RING - 4], 48 * (4 * (p - 1) + 2 * b + 2))
                    nc.scalar.activation(qparts[:, b, 0, :], psZ[:, :], ACT.Copy).then_inc(kq_act, 1)
                if slot == KQ_AT["q"] + 3:
                    act.wait_ge(kq_dve, KQ_DVE.after(g, "qrest1"))
                    nc.scalar.activation(qparts[:, b, 1, :], qrest[:, :], ACT.Copy).then_inc(kq_act, 1)

            def attend(p, b, slot):
                g = 2 * p + b
                for n, name in enumerate(("vf", "vb")):
                    if slot == AT_AT[name] + 1:
                        act.wait_ge(at_pe, AT_PE.after(g, name))
                        nc.scalar.activation(v[:, n, :], psZ[:, :], ACT.Copy).then_inc(at_act, 1)
                n = slot - AT_AT["exp"]
                if 0 <= n < HEADS:
                    if n == 0:
                        act.wait_ge(d_done, D_PAIR * p + D_BEFORE[64 * (b + 1)])
                        act.wait_ge(a_tree, LEVELS * (A_BATCH * p + A_BATCH // 2 * (b + 1)))
                    nc.scalar.activation(P[:, n, :], S[:, b, n, :], ACT.Exp, scale=-1.0 / 8.0,
                                         accum_out=den[:, n:n + 1]).then_inc(at_act, 1)
                for n, name in enumerate(("turna", "turnb")):
                    if slot == AT_AT[name] + 1:
                        act.wait_ge(at_pe, AT_PE.after(g, name))
                        nc.scalar.activation(PT[:, 4 * n:4 * n + 4, :].rearrange("p h t -> p (h t)"), psZ[:, :],
                                             ACT.Copy).then_inc(at_act, 1)
                if slot == AT_AT["gexp"]:
                    act.wait_ge(at_pe, AT_PE.after(g, "pv"))
                    if not (isinstance(g, int) and g == 0):
                        act.wait_ge(at_dve, AT_DVE.after(g - 1, "gate1"))
                    nc.scalar.activation(g1[0:LAT, :], psZ[0:LAT, 0:T], ACT.Exp, scale=-1.702).then_inc(at_act, 1)

            def experts(p, slot):
                if slot == EX_AT["turn"] + 1:
                    act.wait_ge(ex_pe, EX_PE.after(p, "turn"))
                    for b in range(2):
                        nc.scalar.activation(xa[0:LAT, b * T:b * T + T], psZ[b * LAT:b * LAT + LAT, 0:T],
                                             ACT.Copy).then_inc(ex_act, 1)
                if slot == EX_AT["turnoh"] + 1:
                    act.wait_ge(ex_pe, EX_PE.after(p, "turnoh"))
                    nc.scalar.activation(xa[96:128, :], psZ[0:E, 0:2 * T], ACT.Copy).then_inc(ex_act, 1)
                    nc.scalar.activation(ohT[0:E, :], psZ[0:E, 0:2 * T], ACT.Identity, bias=one[0:E, 0:1],
                                         scale=-1.0).then_inc(ex_act, 1)
                for n, name in enumerate(("hida", "hidb")):
                    if slot == EX_AT[name] + 1:
                        act.wait_ge(ex_pe, EX_PE.after(p, name))
                        nc.scalar.activation(hT[:, 2 * n:2 * n + 2, :].rearrange("p a t -> p (a t)"), psZ[:, :],
                                             ACT.Relu).then_inc(ex_act, 1)
                if slot == EX_AT["out"] + 1:
                    act.wait_ge(ex_pe, EX_PE.after(p, "out"))
                    for b in range(2):
                        nc.scalar.activation(fT[b * LAT:b * LAT + LAT, :], psZ[0:LAT, b * T:b * T + T],
                                             ACT.Relu).then_inc(ex_act, 1)

            def prologue():
                act.wait_ge(loaded, LOADED)
                act.wait_ge(ready, READY)
                for s in range(SLOTS):
                    tok(0, s)
                for s in range(SLOTS):
                    norm(0, s)
                for s in range(SLOTS):
                    kq(0, 0, s)
                for s in range(SLOTS):
                    tok(1, s)

            def iteration(i, late=True, tokens=True, ahead=True):
                for s in range(SLOTS):
                    unit(i, s)
                    if late:
                        attend(i - 1, 1, s)
                    kq(i, 1, s)
                    if late:
                        experts(i - 1, s)
                    hand(i, s)
                    if ahead:
                        norm(i + 1, s)
                    attend(i, 0, s - SECOND)
                    if ahead:
                        kq(i + 1, 0, s - SECOND)
                    if tokens:
                        tok(i + 2, s)

            def epilogue():
                for s in range(SLOTS):
                    attend(PAIRS - 1, 1, s)
                    experts(PAIRS - 1, s)

            program(act, prologue, iteration, epilogue)

        @block.vector
        def _(dve):
            def unit(i, slot):
                if shared(slot):
                    return
                b, c, hd = slot // 64, slot // HEADS % CHUNKS, slot % HEADS
                n = D_BEFORE[slot]
                if slot % 64 == 0 and not (isinstance(i, int) and i == 0):
                    dve.wait_ge(at_act, AT_ACT.after(2 * i + b - 2, "exp7"))
                dve.wait_ge(d_made, D_PAIR * i + n + 1)
                nc.vector.tensor_reduce(S[:, b, hd, SB * c:SB * c + SB],
                                        psD[:, n % 2].rearrange("p a s w -> p s a w"), AX.XY, ALU.add,
                                        apply_absolute_value=True).then_inc(d_done, 1)

            def stats(x, name, sm, after):
                for b in range(2):
                    nc.vector.bn_stats(st[name][:, b, :], x[:, b, :]).then_inc(sm, 1)
                dve.wait_ge(sm, after("stat1"))
                nc.vector.memset(spare[:, :], 0.0).then_inc(sm, 1)
                for b in range(2):
                    nc.vector.bn_aggr(mv[name][:, b, :], st[name][:, b, :]).then_inc(sm, 1)
                dve.wait_ge(sm, after("aggr1"))
                nc.vector.tensor_scalar_add(ve[name][:, :], mv[name][:, :, 1], EPS).then_inc(sm, 1)

            def affine(x, name, g, bb, dst, n, p):
                for b in range(2):
                    nc.vector.scalar_tensor_tensor(lt[:, b, 0:n], x[:, b, :], mv[name][:, b, 0:1], g[:, :],
                                                   ALU.subtract, ALU.mult).then_inc(tok_dve, 1)
                dve.wait_ge(tok_pool, TOK_POOL.after(p, "rstd" + name))
                for b in range(2):
                    dve.wait_ge(tok_dve, TOK_DVE.after(p, f"gain{name}{b}"))
                    nc.vector.scalar_tensor_tensor(dst[:, b, 2:2 + J, :].rearrange("p j w -> p (j w)"),
                                                   lt[:, b, 0:n], rstd[name][:, b:b + 1], bb[:, :],
                                                   ALU.mult, ALU.add).then_inc(tok_dve, 1)

            def tok(p, slot):
                def after(name):
                    return lambda s: TOK_DVE.after(p, s[:-1] + name + s[-1])
                if slot == TOK_AT["a"]:
                    dve.wait_ge(x_in, 16 * (p + 1))
                    if not (isinstance(p, int) and p == 0):
                        dve.wait_ge(tok_dve, TOK_DVE.after(p - 1, "h"))
                    stats(xin, "a", tok_dve, after("a"))
                if slot == TOK_AT["a"] + 2:
                    affine(xin, "a", ln0g, ln0b, c1in, 3 * J, p)
                if slot == TOK_AT["b"]:
                    dve.wait_ge(tok_act, TOK_ACT.after(p, "relu1"))
                    stats(y1, "b", tok_dve, after("b"))
                if slot == TOK_AT["b"] + 2:
                    affine(y1, "b", ln0g, ln0b, c2in, 3 * J, p)
                if slot == TOK_AT["c"]:
                    dve.wait_ge(tok_act, TOK_ACT.after(p, "relu2"))
                    stats(y2, "c", tok_dve, after("c"))
                if slot == TOK_AT["c"] + 2:
                    affine(y2, "c", ln1g, ln1b, c3in, 2 * J, p)
                if slot == TOK_AT["d"]:
                    dve.wait_ge(tok_act, TOK_ACT.after(p, "relu3b"))
                    stats(res, "d", tok_dve, after("d"))
                if slot == TOK_AT["d"] + 2:
                    dve.wait_ge(tok_pool, TOK_POOL.after(p, "rstdd"))
                    for b in range(2):
                        nc.vector.tensor_scalar(resn[:, b, :], res[:, b, :], mv["d"][:, b, 0:1], rstd["d"][:, b:b + 1],
                                                ALU.subtract, ALU.mult).then_inc(tok_dve, 1)
                if slot == TOK_AT["out"] + 1:
                    dve.wait_ge(tok_pe, TOK_PE.after(p, "out"))
                    if not (isinstance(p, int) and p == 0):
                        dve.wait_ge(norm_pool, NORM_POOL.after(p - 1, "hx"))
                    nc.vector.tensor_tensor(h[:, :, :], psC[:, 0:2 * LAT].rearrange("p (b w) -> p b w", b=2),
                                            bout[:, :, :], ALU.add).then_inc(tok_dve, 1)

            def norm(p, slot):
                if slot == NORM_AT["stat"]:
                    dve.wait_ge(tok_dve, TOK_DVE.after(p, "h"))
                    stats(h, "n", norm_dve, lambda s: NORM_DVE.after(p, s))
                if slot == NORM_AT["x"]:
                    dve.wait_ge(norm_pool, NORM_POOL.after(p, "rstd"))
                    if not (isinstance(p, int) and p == 0):
                        dve.wait_ge(kq_pool, KQ_POOL.after(2 * p - 1, "k"))
                    for b in range(2):
                        nc.vector.tensor_scalar(x1[:, b, :], h[:, b, :], mv["n"][:, b, 0:1], rstd["n"][:, b:b + 1],
                                                ALU.subtract, ALU.mult).then_inc(norm_dve, 1)

            def kq(p, b, slot):
                g = 2 * p + b
                if slot == KQ_AT["q"] + 2:
                    dve.wait_ge(kq_act, KQ_ACT.after(g, "qpart1"))
                    if not (isinstance(g, int) and g == 0):
                        dve.wait_ge(kq_pool, KQ_POOL.after(g - 1, "qpart3"))
                    nc.vector.tensor_tensor(qrest[:, :], psZ[:, :], qparts[:, b, 0, :],
                                            ALU.subtract).then_inc(kq_dve, 1)

            def attend(p, b, slot):
                g = 2 * p + b
                if slot == AT_AT["den"]:
                    dve.wait_ge(at_act, AT_ACT.after(g, "exp7"))
                    nc.vector.tensor_scalar_add(den1[:, :], den[:, :], 1.0).then_inc(at_dve, 1)
                    dve.wait_ge(at_dve, AT_DVE.after(g, "den"))
                    nc.vector.reciprocal(rden[:, :], den1[:, :]).then_inc(at_dve, 1)
                if slot == AT_AT["gexp"] + 1:
                    dve.wait_ge(at_act, AT_ACT.after(g, "gexp"))
                    nc.vector.tensor_scalar_add(g2[0:LAT, :], g1[0:LAT, :], 1.0).then_inc(at_dve, 1)
                    dve.wait_ge(at_dve, AT_DVE.after(g, "gate1"))
                    nc.vector.reciprocal(g3[0:LAT, :], g2[0:LAT, :]).then_inc(at_dve, 1)
                    dve.wait_ge(at_dve, AT_DVE.after(g, "gate2"))
                    nc.vector.tensor_tensor(gT[0:LAT, b, :], psZ[0:LAT, 0:T], g3[0:LAT, :],
                                            ALU.mult).then_inc(at_dve, 1)

            def experts(p, slot):
                def done(name):
                    return EX_DVE.after(p, name)
                zr = psZ[:, 0:2 * E].rearrange("p (b e) -> p b e", b=2)
                zl = psZ[:, 0:2 * LAT].rearrange("p (b w) -> p b w", b=2)
                if slot == EX_AT["h2"]:
                    dve.wait_ge(ex_pe, EX_PE.after(p, "fan"))
                    dve.wait_ge(hand_act, HAND_ACT.after(p, "hx"))
                    nc.vector.tensor_tensor(h2[:, :, :], zl, hx_late[:, :, :], ALU.add).then_inc(ex_dve, 1)
                    dve.wait_ge(ex_dve, done("h2"))
                    stats(h2, "e", ex_dve, done)
                if slot == EX_AT["x"]:
                    dve.wait_ge(ex_pool, EX_POOL.after(p, "rstd"))
                    for b in range(2):
                        nc.vector.tensor_scalar(x2[:, b, :], h2[:, b, :], mv["e"][:, b, 0:1], rstd["e"][:, b:b + 1],
                                                ALU.subtract, ALU.mult).then_inc(ex_dve, 1)
                if slot == EX_AT["pick"]:
                    dve.wait_ge(ex_pe, EX_PE.after(p, "route"))
                    nc.vector.tensor_reduce(top[:, :], zr, AX.X, ALU.max).then_inc(ex_dve, 1)
                    dve.wait_ge(ex_dve, done("max"))
                    nc.vector.tensor_tensor(eq[:, :, :], zr, top[:, :].unsqueeze(2).broadcast_to([T, 2, E]),
                                            ALU.is_ge).then_inc(ex_dve, 1)
                    dve.wait_ge(ex_dve, done("eq"))
                    nc.vector.tensor_tensor(rev[:, :, :], eq[:, :, :], rank[:, :, :], ALU.mult).then_inc(ex_dve, 1)
                    dve.wait_ge(ex_dve, done("rev"))
                    nc.vector.tensor_reduce(top2[:, :], rev[:, :, :], AX.X, ALU.max).then_inc(ex_dve, 1)
                    dve.wait_ge(ex_dve, done("max2"))
                    nc.vector.tensor_tensor(noh[:, :, :], rev[:, :, :], top2[:, :].unsqueeze(2).broadcast_to([T, 2, E]),
                                            ALU.is_lt).then_inc(ex_dve, 1)
                if slot == EX_AT["back"] + 1:
                    dve.wait_ge(ex_pe, EX_PE.after(p, "back"))
                    if not (isinstance(p, int) and p == 0):
                        dve.wait_ge(stored, 16 * p)
                    nc.vector.tensor_tensor(result[:, :, :], zl, h2[:, :, :], ALU.add).then_inc(ex_dve, 1)

            def prologue():
                for t in (c1in, c2in, c3in, xa, ohT):
                    nc.vector.memset(t[:], 0.0).then_inc(ready, 1)
                nc.vector.memset(be2[32:64, :], 0.0).then_inc(ready, 1)
                nc.vector.memset(be2[64:128, :], 0.0).then_inc(ready, 1)
                nc.vector.memset(we1[64:96, :], 0.0).then_inc(zeroed, 1)
                for t in (x1T, x1T_late):
                    nc.vector.memset(t[64:65, :], 1.0).then_inc(ready, 1)
                nc.vector.memset(gT[64:65, :, :], 1.0).then_inc(ready, 1)
                nc.vector.memset(kT[96:99], -1.0).then_inc(ready, 1)
                nc.vector.memset(half[:, :], -0.5).then_inc(ready, 1)
                nc.vector.memset(one[:, :], 1.0).then_inc(ready, 1)
                dve.wait_ge(ready, 13)
                nc.vector.memset(xa[64:65, :], 1.0).then_inc(ready, 1)
                dve.wait_ge(loaded, LOADED)
                nc.vector.tensor_copy(ident_b[:, :], ident[:, :]).then_inc(ready, 1)
                dve.wait_ge(ready, 15)
                for part in range(3):
                    r = slice(32 * part, 32 * part + 32)
                    ins = nc.vector.tensor_copy(
                        flat[r].rearrange("p r s (n w) -> p (r s n) w", w=32),
                        ident_b[r, r].unsqueeze(1).broadcast_to([32, RING * SB * HW // 32, 32]))
                    ins.then_inc(ready, 1)
                for s in range(SLOTS):
                    tok(0, s)
                for s in range(SLOTS):
                    norm(0, s)
                for s in range(SLOTS):
                    kq(0, 0, s)
                for s in range(SLOTS):
                    tok(1, s)

            def iteration(i, late=True, tokens=True, ahead=True):
                for s in range(SLOTS):
                    unit(i, s)
                    if late:
                        attend(i - 1, 1, s)
                    kq(i, 1, s)
                    if late:
                        experts(i - 1, s)
                    if ahead:
                        norm(i + 1, s)
                    attend(i, 0, s - SECOND)
                    if ahead:
                        kq(i + 1, 0, s - SECOND)
                    if tokens:
                        tok(i + 2, s)

            def epilogue():
                for s in range(SLOTS):
                    attend(PAIRS - 1, 1, s)
                    experts(PAIRS - 1, s)

            program(dve, prologue, iteration, epilogue)

        @block.gpsimd
        def _(pool):
            def unit(i, slot):
                if not shared(slot) or A_BEFORE[slot] % 2 == 0:
                    return
                b, c, hd = slot // 64, slot // HEADS % CHUNKS, slot % HEADS
                n = A_BEFORE[slot]
                heads = SHARED[c]
                first = heads[heads.index(hd) - 1]
                buf = n // 2 % 2
                base = LEVELS * (A_BATCH * i + n // 2)
                pool.wait_ge(a_abs, A_PAIR * i + n + 1)
                t = absd[:, buf]
                lo, hi = (t[:, :, m].rearrange("p u s w -> p u (s w)") for m in range(2))
                nc.gpsimd.tensor_tensor(lo, lo, hi, ALU.add).then_inc(a_tree, 1)
                w = 32
                for level in range(1, LEVELS):
                    w //= 2
                    lo, hi = t[:, :, 0, :, 0:w], t[:, :, 0, :, w:2 * w]
                    dst = lo
                    if level == LEVELS - 1:
                        dst = S[:, b, first:hd + 1:hd - first, SB * c:SB * c + SB].unsqueeze(3)
                        if slot % 64 < 8 and not (isinstance(i, int) and i == 0):
                            pool.wait_ge(at_act, AT_ACT.after(2 * i + b - 2, "exp7"))
                    pool.wait_ge(a_tree, base + level)
                    nc.gpsimd.tensor_tensor(dst, lo, hi, ALU.add).then_inc(a_tree, 1)

            def root(name, dve_sem, value, pool_sem):
                pool.wait_ge(dve_sem, value)
                nc.gpsimd.tensor_tensor(rstd[name][:, :], ve[name][:, :], half[:, :], ALU.pow).then_inc(pool_sem, 1)

            def tok(p, slot):
                for name in "abcd":
                    if slot == TOK_AT[name] + 1:
                        root(name, tok_dve, TOK_DVE.after(p, "eps" + name), tok_pool)

            def norm(p, slot):
                if slot == NORM_AT["rstd"]:
                    root("n", norm_dve, NORM_DVE.after(p, "eps"), norm_pool)
                if slot == NORM_AT["hx"]:
                    pool.wait_ge(norm_dve, NORM_DVE.after(p, "x1"))
                    if not (isinstance(p, int) and p == 0):
                        pool.wait_ge(hand_act, HAND_ACT.after(p - 1, "hx"))
                    nc.gpsimd.tensor_tensor(hx[:, :, :], h[:, :, :], x1[:, :, :], ALU.add).then_inc(norm_pool, 1)

            def kq(p, b, slot):
                g = 2 * p + b
                if slot == KQ_AT["k"]:
                    pool.wait_ge(norm_dve, NORM_DVE.after(p, "x1"))
                    if not (isinstance(g, int) and g == 0):
                        pool.wait_ge(kq_pool, KQ_POOL.after(g - 1, "part3"))
                    nc.gpsimd.tensor_tensor(k[:, :, :, :].rearrange("p h a w -> p h (a w)"),
                                            x1[:, b, :].unsqueeze(1).broadcast_to([T, HEADS, LAT]),
                                            wk[:, :, :], ALU.mult).then_inc(kq_pool, 1)
                if slot == KQ_AT["rest1"]:
                    pool.wait_ge(kq_act, KQ_ACT.after(g, "part1"))
                    nc.gpsimd.tensor_tensor(k[:, :, :, :], k[:, :, :, :], kparts[:, :, :, 0, :],
                                            ALU.subtract).then_inc(kq_pool, 1)
                if slot == KQ_AT["part3"]:
                    pool.wait_ge(kq_act, KQ_ACT.after(g, "part2"))
                    nc.gpsimd.tensor_tensor(kparts[:, :, :, 2, :], k[:, :, :, :], kparts[:, :, :, 1, :],
                                            ALU.subtract).then_inc(kq_pool, 1)
                if slot == KQ_AT["q"] + 4:
                    pool.wait_ge(kq_act, KQ_ACT.after(g, "qpart2"))
                    nc.gpsimd.tensor_tensor(qparts[:, b, 2, :], qrest[:, :], qparts[:, b, 1, :],
                                            ALU.subtract).then_inc(kq_pool, 1)

            def attend(p, b, slot):
                g = 2 * p + b
                for n, name in enumerate(("scalea", "scaleb")):
                    if slot == AT_AT[name]:
                        pool.wait_ge(at_dve, AT_DVE.after(g, "rden"))
                        hs = slice(4 * n, 4 * n + 4)
                        nc.gpsimd.tensor_tensor(P[:, hs, :], P[:, hs, :],
                                                rden[:, hs].unsqueeze(2).broadcast_to([T, 4, T]),
                                                ALU.mult).then_inc(at_pool, 1)

            def experts(p, slot):
                if slot == EX_AT["rstd"]:
                    root("e", ex_dve, EX_DVE.after(p, "eps"), ex_pool)

            def prologue():
                pool.wait_ge(loaded, LOADED)
                pool.wait_ge(ready, READY)
                for s in range(SLOTS):
                    tok(0, s)
                for s in range(SLOTS):
                    norm(0, s)
                for s in range(SLOTS):
                    kq(0, 0, s)
                for s in range(SLOTS):
                    tok(1, s)

            def iteration(i, late=True, tokens=True, ahead=True):
                for s in range(SLOTS):
                    unit(i, s)
                    if late:
                        attend(i - 1, 1, s)
                    kq(i, 1, s)
                    if late:
                        experts(i - 1, s)
                    if ahead:
                        norm(i + 1, s)
                    attend(i, 0, s - SECOND)
                    if ahead:
                        kq(i + 1, 0, s - SECOND)
                    if tokens:
                        tok(i + 2, s)

            def epilogue():
                for s in range(SLOTS):
                    attend(PAIRS - 1, 1, s)
                    experts(PAIRS - 1, s)

            program(pool, prologue, iteration, epilogue)


def lay_out(x, L0_tok_ln0_g, L0_tok_ln0_b, L0_tok_ln1_g, L0_tok_ln1_b, L0_tok_conv1_w, L0_tok_conv1_b,
            L0_tok_conv2_w, L0_tok_conv2_b, L0_tok_conv3_w, L0_tok_conv3_b, L0_tok_out_w, L0_tok_out_b,
            L0_attn_wqv_w, L0_attn_wqv_b, L0_attn_wk, L0_attn_fanin_w, L0_attn_fanin_b, L0_ffn_router_w,
            L0_ffn_router_b, L0_ffn_W1, L0_ffn_b1, L0_ffn_W2, L0_ffn_b2):
    import numpy as np

    def rows(v, *shape):
        return np.broadcast_to(np.reshape(v, (1,) + shape), (T,) + shape)

    def taps(w):
        w = np.transpose(w, (1, 2, 3, 0))
        return w.reshape(w.shape[0], -1, w.shape[3])

    def with_bias(w, b):
        return np.concatenate([w, np.reshape(b, (1, -1))], axis=0)

    shut = np.zeros((E, E, HID), np.float32)
    shut[np.arange(E), np.arange(E), :] = NOT_CHOSEN
    d = {
        "x": np.reshape(x, (x.shape[0], T, 3 * J)),
        "ident": np.eye(T, dtype=np.float32),
        "ln0g": rows(L0_tok_ln0_g, 3 * J), "ln0b": rows(L0_tok_ln0_b, 3 * J),
        "ln1g": rows(L0_tok_ln1_g, 2 * J), "ln1b": rows(L0_tok_ln1_b, 2 * J),
        "ln1g_col": np.reshape(L0_tok_ln1_g, (T, 1)), "ln1b_col": np.reshape(L0_tok_ln1_b, (T, 1)),
        "w1": taps(L0_tok_conv1_w), "w2": taps(L0_tok_conv2_w), "w3": taps(L0_tok_conv3_w),
        "b1": np.reshape(L0_tok_conv1_b, (T, 1)), "b2": np.reshape(L0_tok_conv2_b, (T, 1)),
        "b3": np.transpose(np.reshape(L0_tok_conv3_b, (2, T))),
        "wout": L0_tok_out_w,
        "bout": np.broadcast_to(np.reshape(L0_tok_out_b, (1, 1, LAT)), (T, 2, LAT)),
        "wqv": with_bias(np.transpose(L0_attn_wqv_w), L0_attn_wqv_b),
        "wk": rows(L0_attn_wk, HEADS, LAT),
        "wfan": with_bias(np.transpose(L0_attn_fanin_w), L0_attn_fanin_b),
        "wroute": with_bias(np.transpose(L0_ffn_router_w), L0_ffn_router_b),
        "we1": with_bias(np.reshape(np.transpose(L0_ffn_W1, (1, 0, 2)), (LAT, E * HID)), L0_ffn_b1),
        "shut": np.reshape(shut, (E, E * HID)),
        "we2": np.transpose(np.reshape(L0_ffn_W2, (4, T, LAT)), (1, 0, 2)),
        "be2": L0_ffn_b2,
        "rank": np.broadcast_to((E - np.arange(E, dtype=np.float32)).reshape(1, 1, E), (T, 2, E)),
    }
    return {name: np.ascontiguousarray(v) for name, v in d.items()}


def kernel(**inputs):
    import numpy as np
    from concourse import bacc, mybir as mb
    from concourse.bass_utils import run_bass_kernel_spmd

    arrays = lay_out(**{name: np.asarray(v) for name, v in inputs.items()})
    nc = bacc.Bacc("TRN2", target_bir_lowering=False, num_devices=1)
    aps = {name: nc.dram_tensor("in_" + name, v.shape, mb.dt.from_np(v.dtype), kind="ExternalInput").ap()
           for name, v in arrays.items()}
    out = nc.dram_tensor("out_h", (arrays["x"].shape[0], T, LAT), F32, kind="ExternalOutput").ap()
    vit_tower(nc, aps, out)
    r = run_bass_kernel_spmd(nc, [{"in_" + name: v for name, v in arrays.items()}], core_ids=[0])
    return r.results[0]["out_h"]
```

```python
from contextlib import ExitStack

import concourse.bass as bass
from concourse import mybir

F32 = mybir.dt.float32
BF16 = mybir.dt.bfloat16
ALU = mybir.AluOpType
ACT = mybir.ActivationFunctionType
AX = mybir.AxisListType

T = 128
J = 64
LAT = 64
HEADS = 8
HW = HEADS * LAT
E, HID = 32, 16
EPS = 1e-5
SB = 16
CHUNKS = T // SB
RING = 4
SLOTS = 2 * CHUNKS * HEADS
NOT_CHOSEN = -1e30

SHARED = [(2, 5), (3, 5), (2, 5), (1, 5), (2, 5), (1, 5), (2, 5), (0, 2, 4, 6),
          (), (1, 5), (2, 5), (1, 5), (2, 5), (1, 4, 5, 6), (2, 5), (0, 2, 4, 6)]
assert len(SHARED) == 2 * CHUNKS and all(len(x) % 2 == 0 and HEADS - 1 not in x for x in SHARED)
A_PAIR = sum(len(x) for x in SHARED)
TREES = A_PAIR // 2
D_PAIR = SLOTS - A_PAIR
PLACES = 3
GROUPS = 3
assert TREES % GROUPS == 0
LEVELS = 6


def shared(slot):
    return slot % HEADS in SHARED[slot // HEADS]


D_BEFORE = [sum(not shared(x) for x in range(s)) for s in range(SLOTS + 1)]
A_BEFORE = [sum(shared(x) for x in range(s)) for s in range(SLOTS + 1)]


class Steps:

    def __init__(self, names):
        self.names = names.split()

    def after(self, n, name):
        return n * len(self.names) + (self.names.index(name) + 1)


TOK_PE = Steps("conv1 conv2 conv3 turn out")
TOK_ACT = Steps("relu1 relu2 relu3a relu3b turned")
LN = "stat{0}0 stat{0}1 wait{0} aggr{0}0 aggr{0}1 eps{0} "
LN_APPLY = "gain{0}0 gain{0}1 shift{0}0 shift{0}1 "
TOK_DVE = Steps("".join(LN.format(x) + LN_APPLY.format(x) for x in "abc") + LN.format("d") + "norm0 norm1 h")
TOK_POOL = Steps("rstda rstdb rstdc rstdd")
NORM_DVE = Steps("stat0 stat1 wait aggr0 aggr1 eps x0 x1")
NORM_POOL = Steps("rstd hx")
NORM_PE = Steps("turn")
NORM_ACT = Steps("turned0 turned")
HAND_ACT = Steps("xT hx")
K_POOL = Steps("k rest1 part3")
K_ACT = Steps("part1 part2 kTa kTb")
K_PE = Steps("kTa kTb")
Q_PE = Steps("q")
Q_ACT = Steps("qpart1 qpart2")
Q_DVE = Steps("qrest1")
Q_POOL = Steps("qpart3")
AT_PE = Steps("vf vb turna turnb pv")
AT_ACT = Steps("vf vb exp0 exp1 exp2 exp3 exp4 exp5 exp6 exp7 scale0 scale1 scale2 scale3 scale4 scale5 scale6 scale7 turneda turnedb half tanh")
AT_DVE = Steps("den rden sum gate")
EX_PE = Steps("fan turn route turnoh hida hidb out back")
EX_DVE = Steps("h2 stat0 stat1 wait aggr0 aggr1 eps x0 x1 max eq rev max2 noh result")
EX_POOL = Steps("rstd")
EX_ACT = Steps("turned0 turned noh oh relua relub relu0 relu")

def spread(slot, at, length, count):
    return [n for n in range(count) if at + n * length // count == slot]


KQ_AT = dict(k=0, part1=11, rest1=12, part2=24, part3=25, kTa=44, kTb=46, q=10, qpart1=11, qrest1=14,
             qpart2=16, qpart3=16)
AT_AT = dict(vf=2, vb=3, exp=8, exp_len=9, den=19, scale=19, scale_len=7, turna=25, turnb=27, pv=30, pv_len=8,
             half=36, sum=37, tanh=43, gate=41)
SECOND = 66
EX_AT = dict(fan=43, h2=42, rstd=47, x=50, turn=52, route=55, pick=56, turnoh=58, hida=60, hidb=63, out=65, back=72)
NORM_AT = dict(stat=19, rstd=20, x=30, turn=42, hx=53)
HAND_AT = dict(xT=31, hx=46)
TOK_AT = dict(a=2, conv1=14, len1=15, b=35, conv2=46, len2=10, c=58, conv3=70, len3=22, d=91, turn=103,
              out=104, root=0, gap=9)


def vit_tower(nc, a, out):
    PAIRS = a["x"].shape[0] // 2
    x_v = a["x"].rearrange("b t f -> t b f")
    out_v = out.rearrange("b t w -> t b w")

    with ExitStack() as ctx:
        def sb(name, shape, dt=F32):
            return ctx.enter_context(nc.sbuf_tensor(name, shape, dt))

        def sem(name):
            return ctx.enter_context(nc.semaphore(name))

        ident = sb("ident", [T, T])
        ident_b = sb("ident_b", [T, T], BF16)
        ln0g = sb("ln0g", [T, 3 * J])
        ln0b = sb("ln0b", [T, 3 * J])
        ln1g = sb("ln1g", [T, 2 * J])
        ln1b = sb("ln1b", [T, 2 * J])
        ln1g_col = sb("ln1g_col", [T, 1])
        ln1b_col = sb("ln1b_col", [T, 1])
        w1 = sb("w1", [T, 15, T])
        w2 = sb("w2", [T, 10, T])
        w3 = sb("w3", [T, 10, 2 * T])
        b1 = sb("b1", [T, 1])
        b2 = sb("b2", [T, 1])
        b3 = sb("b3", [T, 2])
        wout = sb("wout", [T, LAT])
        bout = sb("bout", [T, 2, LAT])
        wqv = sb("wqv", [T, 3 * HW])
        wk = sb("wk", [T, HEADS, LAT])
        wfan = sb("wfan", [T, LAT])
        wroute = sb("wroute", [T, E])
        we1 = sb("we1", [T, E * HID])
        we2 = sb("we2", [T, 4, LAT])
        be2 = sb("be2", [T, LAT])
        rank = sb("rank", [T, 2, E])
        half = sb("half", [T, 2])
        one = sb("one", [T, 1])
        spare = sb("spare", [T, 1])

        xin = sb("xin", [T, 2, 3 * J])
        lt = sb("lt", [T, 2, 3 * J])
        c1in = sb("c1in", [T, 2, J + 4, 3])
        c2in = sb("c2in", [T, 2, J + 4, 3])
        c3in = sb("c3in", [T, 2, J + 4, 2])
        y1 = sb("y1", [T, 2, 3 * J])
        y2 = sb("y2", [T, 2, 2 * J])
        res = sb("res", [T, 2, 2 * J])
        resn = sb("resn", [T, 2, 2 * J])
        resT = sb("resT", [T, 2, T])
        st = {k: sb("st" + k, [T, 2, 6]) for k in "abcdne"}
        mv = {k: sb("mv" + k, [T, 2, 2]) for k in "abcdne"}
        ve = {k: sb("ve" + k, [T, 2]) for k in "abcdne"}
        rstd = {k: sb("rstd" + k, [T, 2]) for k in "abcdne"}
        h = sb("h", [T, 2, LAT])
        x1 = sb("x1", [T, 2, LAT])
        x1T = sb("x1T", [T, 2 * T])
        x1T_late = sb("x1T_late", [T, 2 * T])
        hx = sb("hx", [T, 2, LAT])
        hx_late = sb("hx_late", [T, 2, LAT])
        k = sb("k", [T, HEADS, 2, 32])
        kparts = sb("kparts", [T, HEADS, 2, 3, 32], BF16)
        kT = sb("kT", [T, 2, HEADS, 2, T], BF16)
        qrest = sb("qrest", [T, HW])
        qparts = sb("qparts", [T, 2, 3, HW], BF16)
        flat = sb("flat", [T, RING, SB, HW], BF16)
        absd = sb("absd", [T, GROUPS, 2, 2, SB, 32])
        S = sb("S", [T, 2, HEADS, T])
        P = sb("P", [T, HEADS, 2, T])
        den = sb("den", [T, HEADS])
        den1 = sb("den1", [T, HEADS])
        rden = sb("rden", [T, HEADS])
        v = sb("v", [T, HEADS, 2, LAT])
        o_half = sb("o_half", [T, T])
        o = sb("o", [T, T])
        th = sb("th", [T, T])
        gT = sb("gT", [T, 2, T])
        h2 = sb("h2", [T, 2, LAT])
        x2 = sb("x2", [T, 2, LAT])
        xa = sb("xa", [T, 2 * T])
        top = sb("top", [T, 2])
        eq = sb("eq", [T, 2, E])
        rev = sb("rev", [T, 2, E])
        top2 = sb("top2", [T, 2])
        noh = sb("noh", [T, 2, E])
        ohT = sb("ohT", [T, 2 * T])
        hT = sb("hT", [T, 4, 2 * T])
        fT = sb("fT", [T, T])
        result = sb("result", [T, 2, LAT])

        psU = ctx.enter_context(nc.psum_tensor("psU", [T, PLACES, 2, SB, 32], F32))
        psC = ctx.enter_context(nc.psum_tensor("psC", [T, 512], F32))
        psZ = ctx.enter_context(nc.psum_tensor("psZ", [T, 512], F32))
        psZb = psZ[:, :].bitcast(BF16)

        loaded_first = sem("loaded_first")
        loaded = sem("loaded")
        ready = sem("ready")
        filled = sem("filled")
        zeroed = sem("zeroed")
        x_in = sem("x_in")
        stored = sem("stored")
        flat_in = [sem(f"flat_in{n}") for n in range(RING)]
        d_made = sem("d_made")
        d_done = sem("d_done")
        a_made = sem("a_made")
        a_abs = sem("a_abs")
        a_tree = sem("a_tree")
        tok_pe, tok_act, tok_dve, tok_pool = (sem("tok_" + e) for e in ("pe", "act", "dve", "pool"))
        norm_pe, norm_act, norm_dve, norm_pool = (sem("norm_" + e) for e in ("pe", "act", "dve", "pool"))
        hand_act = sem("hand_act")
        keys_pe, keys_act, keys_pool = (sem("keys_" + e) for e in ("pe", "act", "pool"))
        queries_pe, queries_act, queries_dve, queries_pool = (sem("queries_" + e) for e in ("pe", "act", "dve", "pool"))
        at_pe, at_act, at_dve = (sem("at_" + e) for e in ("pe", "act", "dve"))
        ex_pe, ex_act, ex_dve, ex_pool = (sem("ex_" + e) for e in ("pe", "act", "dve", "pool"))

        first = [(ident, a["ident"]), (ln0g, a["ln0g"]), (ln0b, a["ln0b"]), (w1, a["w1"]), (b1, a["b1"])]
        weights = [
            (w2, a["w2"]), (b2, a["b2"]), (ln1g, a["ln1g"]), (ln1b, a["ln1b"]), (w3, a["w3"]), (b3, a["b3"]),
            (ln1g_col, a["ln1g_col"]), (ln1b_col, a["ln1b_col"]), (wout, a["wout"]), (bout, a["bout"]),
            (wk, a["wk"]), (rank, a["rank"]), (we2, a["we2"]),
        ]
        parts_of = [
            (wqv[0:65, :], a["wqv"]), (wfan[0:65, :], a["wfan"]), (wroute[0:65, :], a["wroute"]),
            (we1[0:65, :], a["we1"]), (we1[96:128, :], a["shut"]), (be2[0:E, :], a["be2"]),
        ]
        READY = 15
        FIRST = 16 * len(first)
        LOADED = 16 * (len(weights) + len(parts_of))
        block = ctx.enter_context(nc.Block())

        def program(eng, prologue, iteration, epilogue):
            prologue()
            iteration(0, late=False)
            with eng.Fori(1, PAIRS - 2) as i:
                iteration(i)
            iteration(PAIRS - 2, tokens=False)
            iteration(PAIRS - 1, tokens=False, ahead=False)
            epilogue()

        @block.sync
        def _(sp):
            sp.dma_start(xin[:, :, :], x_v[:, 0:2, :]).then_inc(x_in, 16)
            for dst, src in first:
                sp.dma_start(dst[:], src).then_inc(loaded_first, 16)
            for dst, src in weights:
                sp.dma_start(dst[:], src).then_inc(loaded, 16)
            sp.wait_ge(zeroed, 1)
            for dst, src in parts_of:
                sp.dma_start(dst, src).then_inc(loaded, 16)

            def load_x(p):
                sp.wait_ge(tok_dve, TOK_DVE.after(p - 1, "gaina1"))
                sp.dma_start(xin[:, :, :], x_v[:, bass.ds(2 * p, 2), :]).then_inc(x_in, 16)

            def load_flat(batch, b, c):
                for part in range(3):
                    sp.dma_start(flat[96 + part:97 + part, c % RING, :, :],
                                 qparts[SB * c:SB * c + SB, b, part, :]).then_inc(flat_in[c % RING], 16)

            def store(p):
                sp.wait_ge(ex_dve, EX_DVE.after(p, "result"))
                sp.dma_start(out_v[:, bass.ds(2 * p, 2), :], result[:, :, :]).then_inc(stored, 16)

            def prologue():
                load_x(1)
                sp.wait_ge(queries_pool, Q_POOL.after(0, "qpart3"))
                for c in range(RING):
                    load_flat(0, 0, c)

            def iteration(i, late=True, tokens=True, ahead=True):
                if tokens:
                    load_x(i + 2)
                for j in range(2 * CHUNKS):
                    c = j + RING
                    if c < 2 * CHUNKS or ahead:
                        sp.wait_ge(d_made, D_PAIR * i + D_BEFORE[HEADS * (j + 1)])
                        load_flat(2 * i + c // CHUNKS, c // CHUNKS % 2, c % CHUNKS)
                    if j == 10 and late:
                        store(i - 1)

            def epilogue():
                store(PAIRS - 1)
                sp.wait_ge(stored, 16 * PAIRS)

            program(sp, prologue, iteration, epilogue)

        @block.tensor
        def _(pe):
            bank = [None]

            def take_bank(reader, value):
                if bank[0] is not None:
                    pe.wait_ge(*bank[0])
                bank[0] = (reader, value)

            def unit(i, slot):
                b, c, hd = slot // 64, slot // HEADS % CHUNKS, slot % HEADS
                if slot == 0 and isinstance(i, int) and i == 0:
                    pe.wait_ge(filled, 3)
                if slot % 64 == 0:
                    pe.wait_ge(keys_act, K_ACT.after(2 * i + b, "kTb"))
                if hd == 0:
                    pe.wait_ge(flat_in[c % RING], 48 * (4 * i + (slot // HEADS) // RING + 1))
                if slot % 64 == 64 - RING * HEADS and not (isinstance(i, int) and 2 * i + b + 1 == 2 * PAIRS):
                    pe.wait_ge(queries_pool, Q_POOL.after(2 * i + b + 1, "qpart3"))
                if slot >= PLACES:
                    before, j = slot - PLACES, i
                else:
                    before, j = max(s for s in range(SLOTS) if s % PLACES == slot), i - 1
                if isinstance(j, int) and j < 0:
                    pass
                elif shared(before):
                    pe.wait_ge(a_abs, A_PAIR * j + A_BEFORE[before + 1])
                else:
                    pe.wait_ge(d_done, D_PAIR * j + D_BEFORE[before + 1])
                dst, made = psU[:, slot % PLACES], a_made if shared(slot) else d_made
                for hf in range(2):
                    lo = hd * LAT + hf * 32
                    mm = nc.tensor.matmul(dst[:, hf], kT[0:99, b, hd, hf, :],
                                          flat[0:99, c % RING, :, lo:lo + 32], start=True, stop=True)
                mm.then_inc(made, 1)

            def tok(p, slot):
                for n in spread(slot, TOK_AT["conv1"], TOK_AT["len1"], 15):
                    dy, m = n // 3, n % 3
                    dx, o, w0, wn = ((1, 0, 0, 3), (0, 1, 0, 2), (2, 0, 1, 2))[m]
                    if n == 0:
                        pe.wait_ge(tok_dve, TOK_DVE.after(p, "shifta1"))
                        if not (isinstance(p, int) and p == 0):
                            pe.wait_ge(tok_dve, TOK_DVE.after(p - 1, "h"))
                    o_v = psC[:, 0:6 * J].rearrange("p (b j w) -> p b j w", b=2, w=3)
                    mm = nc.tensor.matmul(o_v[:, :, :, o:o + wn], w1[:, 3 * dy + dx, :],
                                          c1in[:, :, dy:dy + J, w0:w0 + wn], start=(n == 0), stop=(n == 14))
                    if n == 14:
                        mm.then_inc(tok_pe, 1)
                for n in spread(slot, TOK_AT["conv2"], TOK_AT["len2"], 10):
                    if n == 0:
                        pe.wait_ge(tok_act, TOK_ACT.after(p, "relu1"))
                        pe.wait_ge(tok_dve, TOK_DVE.after(p, "shiftb1"))
                    dy, dx = n // 2, n % 2
                    mm = nc.tensor.matmul(psC[:, 0:4 * J].rearrange("p (b j w) -> p b j w", b=2, w=2),
                                          w2[:, n, :], c2in[:, :, dy:dy + J, dx:dx + 2],
                                          start=(n == 0), stop=(n == 9))
                    if n == 9:
                        mm.then_inc(tok_pe, 1)
                for n in spread(slot, TOK_AT["conv3"], TOK_AT["len3"], 20):
                    if n == 0:
                        pe.wait_ge(tok_act, TOK_ACT.after(p, "relu2"))
                        pe.wait_ge(tok_dve, TOK_DVE.after(p, "shiftc1"))
                    hf, m = n // 10, n % 10
                    dy, dx = m // 2, m % 2
                    mm = nc.tensor.matmul(psC[:, hf * T:hf * T + T].rearrange("p (b j) -> p b j", b=2),
                                          w3[:, m, hf * T:hf * T + T], c3in[:, :, dy:dy + J, dx],
                                          start=(m == 0), stop=(m == 9))
                    if n == 19:
                        mm.then_inc(tok_pe, 1)
                if slot == TOK_AT["turn"]:
                    pe.wait_ge(tok_act, TOK_ACT.after(p, "relu3b"))
                    pe.wait_ge(tok_dve, TOK_DVE.after(p, "norm1"))
                    for b in range(2):
                        mm = nc.tensor.transpose(psC[:, b * T:b * T + T], resn[:, b, :], ident[:, :])
                    mm.then_inc(tok_pe, 1)
                if slot == TOK_AT["out"]:
                    pe.wait_ge(tok_act, TOK_ACT.after(p, "turned"))
                    for b in range(2):
                        mm = nc.tensor.matmul(psC[:, b * LAT:b * LAT + LAT], resT[:, b, :], wout[:, :],
                                              start=True, stop=True)
                    mm.then_inc(tok_pe, 1)

            def norm(p, slot):
                if slot == NORM_AT["turn"]:
                    take_bank(norm_act, NORM_ACT.after(p, "turned"))
                    pe.wait_ge(norm_dve, NORM_DVE.after(p, "x1"))
                    nc.tensor.transpose(psZ[:, 0:T], x1[:, :, :].rearrange("p b w -> p (b w)"),
                                        ident[:, :]).then_inc(norm_pe, 1)

            def kq(p, b, slot):
                g = 2 * p + b
                for n, name in enumerate(("kTa", "kTb")):
                    if slot == KQ_AT[name]:
                        take_bank(keys_act, K_ACT.after(g, name))
                        pe.wait_ge(keys_pool, K_POOL.after(g, "part3"))
                        for m in range(8):
                            mm = nc.tensor.transpose(
                                psZb[0:96, m * T:m * T + T],
                                kparts[:, 4 * n + m // 2, m % 2, :, :].rearrange("p a w -> p (a w)"), ident_b[:, :])
                        mm.then_inc(keys_pe, 1)
                if slot == KQ_AT["q"]:
                    take_bank(queries_dve, Q_DVE.after(g, "qrest1"))
                    pe.wait_ge(norm_act, NORM_ACT.after(p, "turned"))
                    nc.tensor.matmul(psZ[:, :], x1T[0:65, b * T:b * T + T], wqv[0:65, 0:HW],
                                     start=True, stop=True).then_inc(queries_pe, 1)

            def attend(p, b, slot):
                g = 2 * p + b
                for n, name in enumerate(("vf", "vb")):
                    if slot == AT_AT[name]:
                        take_bank(at_act, AT_ACT.after(g, name))
                        pe.wait_ge(hand_act, HAND_ACT.after(p, "xT"))
                        nc.tensor.matmul(psZ[:, :], x1T_late[0:65, b * T:b * T + T],
                                         wqv[0:65, (1 + n) * HW:(2 + n) * HW],
                                         start=True, stop=True).then_inc(at_pe, 1)
                for n, name in enumerate(("turna", "turnb")):
                    if slot == AT_AT[name]:
                        take_bank(at_act, AT_ACT.after(g, ("turneda", "turnedb")[n]))
                        pe.wait_ge(at_act, AT_ACT.after(g, ("scale3", "scale7")[n]))
                        for m in range(4):
                            mm = nc.tensor.transpose(psZ[:, m * T:m * T + T], P[:, 4 * n + m, 0, :], ident[:, :])
                        mm.then_inc(at_pe, 1)
                for n in spread(slot, AT_AT["pv"], AT_AT["pv_len"], HEADS):
                    if n == 0:
                        take_bank(at_dve, AT_DVE.after(g, "sum"))
                        pe.wait_ge(at_act, AT_ACT.after(g, "turnedb"))
                    mm = nc.tensor.matmul(psZ[:, 0:2 * T], v[:, n, :, :].rearrange("p a w -> p (a w)"),
                                          P[:, n, :, :].rearrange("p a t -> p (a t)"),
                                          start=(n == 0), stop=(n == HEADS - 1))
                    if n == HEADS - 1:
                        mm.then_inc(at_pe, 1)

            def experts(p, slot):
                if slot == EX_AT["fan"]:
                    take_bank(ex_dve, EX_DVE.after(p, "h2"))
                    pe.wait_ge(at_dve, AT_DVE.after(2 * p + 1, "gate"))
                    for b in range(2):
                        mm = nc.tensor.matmul(psZ[:, b * LAT:b * LAT + LAT], gT[0:65, b, :], wfan[0:65, :],
                                              start=True, stop=True)
                    mm.then_inc(ex_pe, 1)
                if slot == EX_AT["turn"]:
                    take_bank(ex_act, EX_ACT.after(p, "turned"))
                    pe.wait_ge(ex_dve, EX_DVE.after(p, "x1"))
                    nc.tensor.transpose(psZ[:, 0:T], x2[:, :, :].rearrange("p b w -> p (b w)"),
                                        ident[:, :]).then_inc(ex_pe, 1)
                if slot == EX_AT["route"]:
                    take_bank(ex_dve, EX_DVE.after(p, "eq"))
                    for b in range(2):
                        mm = nc.tensor.matmul(psZ[:, b * E:b * E + E], xa[0:65, b * T:b * T + T], wroute[0:65, :],
                                              start=True, stop=True)
                    mm.then_inc(ex_pe, 1)
                if slot == EX_AT["turnoh"]:
                    take_bank(ex_act, EX_ACT.after(p, "oh"))
                    pe.wait_ge(ex_dve, EX_DVE.after(p, "noh"))
                    for b in range(2):
                        mm = nc.tensor.transpose(psZ[0:E, b * T:b * T + T], noh[:, b, :], ident[:, :])
                    mm.then_inc(ex_pe, 1)
                for n, name in enumerate(("hida", "hidb")):
                    if slot == EX_AT[name]:
                        take_bank(ex_act, EX_ACT.after(p, ("relua", "relub")[n]))
                        for m in range(2):
                            q = 2 * n + m
                            mm = nc.tensor.matmul(psZ[:, m * 256:m * 256 + 256], we1[:, q * T:q * T + T], xa[:, :],
                                                  start=True, stop=True)
                        mm.then_inc(ex_pe, 1)
                if slot == EX_AT["out"]:
                    take_bank(ex_act, EX_ACT.after(p, "relu"))
                    for q in range(4):
                        nc.tensor.matmul(psZ[0:LAT, 0:256], we2[:, q, :], hT[:, q, :], start=(q == 0), stop=False)
                    nc.tensor.matmul(psZ[0:LAT, 0:256], be2[:, :], ohT[:, :], start=False,
                                     stop=True).then_inc(ex_pe, 1)
                if slot == EX_AT["back"]:
                    take_bank(ex_dve, EX_DVE.after(p, "result"))
                    nc.tensor.transpose(psZ[:, 0:2 * LAT], fT[:, :], ident[:, :]).then_inc(ex_pe, 1)

            def prologue():
                pe.wait_ge(loaded_first, FIRST)
                pe.wait_ge(ready, READY)
                for s in range(SLOTS):
                    if s == TOK_AT["conv2"]:
                        pe.wait_ge(loaded, LOADED)
                    tok(0, s)
                for s in range(SLOTS):
                    norm(0, s)
                    kq(0, 0, s - SECOND)
                    tok(1, s)

            def iteration(i, late=True, tokens=True, ahead=True):
                if not isinstance(i, int) or i > 0:
                    if KQ_AT["kTb"] > AT_AT["pv"]:
                        bank[0] = (keys_act, K_ACT.after(2 * i, "kTb"))
                    else:
                        bank[0] = (at_dve, AT_DVE.after(2 * i - 2, "sum"))
                for s in range(SLOTS):
                    unit(i, s)
                    if late:
                        attend(i - 1, 1, s)
                    kq(i, 1, s)
                    if late:
                        experts(i - 1, s)
                    if ahead:
                        norm(i + 1, s)
                    attend(i, 0, s - SECOND)
                    if ahead:
                        kq(i + 1, 0, s - SECOND)
                    if tokens:
                        tok(i + 2, s)

            def epilogue():
                for s in range(SLOTS):
                    attend(PAIRS - 1, 1, s)
                    experts(PAIRS - 1, s)

            program(pe, prologue, iteration, epilogue)

        @block.scalar
        def _(act):
            def unit(i, slot):
                if not shared(slot):
                    return
                n = A_BEFORE[slot]
                act.wait_ge(a_made, A_PAIR * i + n + 1)
                if n % 2 == 0 and not (isinstance(i, int) and i == 0 and n < 2 * GROUPS):
                    act.wait_ge(a_tree, LEVELS * (TREES * i + n // 2 - (GROUPS - 1)))
                nc.scalar.activation(absd[:, n // 2 % GROUPS, n % 2], psU[:, slot % PLACES], ACT.Abs).then_inc(a_abs, 1)

            def tok(p, slot):
                if slot == TOK_AT["conv1"] + TOK_AT["len1"]:
                    act.wait_ge(tok_pe, TOK_PE.after(p, "conv1"))
                    nc.scalar.activation(y1[:, :, :], psC[:, 0:6 * J].rearrange("p (b f) -> p b f", b=2), ACT.Relu,
                                         bias=b1[:, 0:1]).then_inc(tok_act, 1)
                if slot == TOK_AT["conv2"] + TOK_AT["len2"]:
                    act.wait_ge(tok_pe, TOK_PE.after(p, "conv2"))
                    nc.scalar.activation(y2[:, :, :], psC[:, 0:4 * J].rearrange("p (b f) -> p b f", b=2), ACT.Relu,
                                         bias=b2[:, 0:1]).then_inc(tok_act, 1)
                if slot == TOK_AT["conv3"] + TOK_AT["len3"]:
                    act.wait_ge(tok_pe, TOK_PE.after(p, "conv3"))
                    for hf in range(2):
                        nc.scalar.activation(res[:, :, hf * J:hf * J + J],
                                             psC[:, hf * T:hf * T + T].rearrange("p (b j) -> p b j", b=2), ACT.Relu,
                                             bias=b3[:, hf:hf + 1]).then_inc(tok_act, 1)
                if slot == TOK_AT["turn"] + 1:
                    act.wait_ge(tok_pe, TOK_PE.after(p, "turn"))
                    nc.scalar.activation(resT[:, :, :], psC[:, 0:2 * T].rearrange("p (b t) -> p b t", b=2),
                                         ACT.Identity, bias=ln1b_col[:, 0:1], scale=ln1g_col[:, 0:1])\
                        .then_inc(tok_act, 1)

            def norm(p, slot):
                if slot == NORM_AT["turn"] + 1:
                    act.wait_ge(norm_pe, NORM_PE.after(p, "turn"))
                    if not (isinstance(p, int) and p == 0):
                        act.wait_ge(hand_act, HAND_ACT.after(p - 1, "xT"))
                    for b in range(2):
                        nc.scalar.activation(x1T[0:LAT, b * T:b * T + T], psZ[b * LAT:b * LAT + LAT, 0:T],
                                             ACT.Copy).then_inc(norm_act, 1)

            def hand(p, slot):
                if slot == HAND_AT["xT"]:
                    if not (isinstance(p, int) and p == 0):
                        act.wait_ge(at_pe, AT_PE.after(2 * p - 1, "vb"))
                    act.wait_ge(norm_act, NORM_ACT.after(p, "turned"))
                    nc.scalar.activation(x1T_late[0:LAT, :], x1T[0:LAT, :], ACT.Copy).then_inc(hand_act, 1)
                if slot == HAND_AT["hx"]:
                    if not (isinstance(p, int) and p == 0):
                        act.wait_ge(ex_dve, EX_DVE.after(p - 1, "h2"))
                    act.wait_ge(norm_pool, NORM_POOL.after(p, "hx"))
                    nc.scalar.activation(hx_late[:, :, :], hx[:, :, :], ACT.Copy).then_inc(hand_act, 1)

            def kq(p, b, slot):
                g = 2 * p + b
                if slot == KQ_AT["part1"]:
                    act.wait_ge(keys_pool, K_POOL.after(g, "k"))
                    nc.scalar.activation(kparts[:, :, :, 0, :], k[:, :, :, :], ACT.Copy).then_inc(keys_act, 1)
                if slot == KQ_AT["part2"]:
                    act.wait_ge(keys_pool, K_POOL.after(g, "rest1"))
                    nc.scalar.activation(kparts[:, :, :, 1, :], k[:, :, :, :], ACT.Copy).then_inc(keys_act, 1)
                for n, name in enumerate(("kTa", "kTb")):
                    if slot == KQ_AT[name] + 1:
                        act.wait_ge(keys_pe, K_PE.after(g, name))
                        if not (isinstance(p, int) and p == 0):
                            act.wait_ge(d_made, D_PAIR * (p - 1) + D_BEFORE[64 * (b + 1)])
                        nc.scalar.activation(kT[0:96, b, 4 * n:4 * n + 4, :, :].rearrange("p h a t -> p (h a t)"),
                                             psZb[0:96, 0:8 * T], ACT.Copy).then_inc(keys_act, 1)
                if slot == KQ_AT["qpart1"]:
                    act.wait_ge(queries_pe, Q_PE.after(g, "q"))
                    if not (isinstance(p, int) and p == 0):
                        act.wait_ge(flat_in[RING - 1], 48 * (4 * (p - 1) + 2 * b + 2))
                        act.wait_ge(flat_in[RING - 2], 48 * (4 * (p - 1) + 2 * b + 2))
                        act.wait_ge(flat_in[RING - 3], 48 * (4 * (p - 1) + 2 * b + 2))
                        act.wait_ge(flat_in[RING - 4], 48 * (4 * (p - 1) + 2 * b + 2))
                    nc.scalar.activation(qparts[:, b, 0, :], psZ[:, :], ACT.Copy).then_inc(queries_act, 1)
                if slot == KQ_AT["qpart2"]:
                    act.wait_ge(queries_dve, Q_DVE.after(g, "qrest1"))
                    nc.scalar.activation(qparts[:, b, 1, :], qrest[:, :], ACT.Copy).then_inc(queries_act, 1)

            def attend(p, b, slot):
                g = 2 * p + b
                for n, name in enumerate(("vf", "vb")):
                    if slot == AT_AT[name] + 1:
                        act.wait_ge(at_pe, AT_PE.after(g, name))
                        nc.scalar.activation(v[:, :, 1 - n, :], psZ[:, :].rearrange("p (h w) -> p h w", h=HEADS),
                                             ACT.Copy).then_inc(at_act, 1)
                for n in spread(slot, AT_AT["exp"], AT_AT["exp_len"], HEADS):
                    if n == 0:
                        act.wait_ge(d_done, D_PAIR * p + D_BEFORE[64 * (b + 1)])
                        act.wait_ge(a_tree, LEVELS * (TREES * p + A_BEFORE[64 * (b + 1)] // 2))
                    nc.scalar.activation(P[:, n, 0, :], S[:, b, n, :], ACT.Exp, scale=-1.0 / 8.0,
                                         accum_out=den[:, n:n + 1]).then_inc(at_act, 1)
                for n in spread(slot, AT_AT["scale"], AT_AT["scale_len"], HEADS):
                    if n == 0:
                        act.wait_ge(at_dve, AT_DVE.after(g, "rden"))
                    nc.scalar.activation(P[:, n, 0, :], P[:, n, 0, :], ACT.Copy, scale=rden[:, n:n + 1]).then_inc(at_act, 1)
                for n, name in enumerate(("turna", "turnb")):
                    if slot == AT_AT[name] + 1:
                        act.wait_ge(at_pe, AT_PE.after(g, name))
                        nc.scalar.activation(P[:, 4 * n:4 * n + 4, 1, :],
                                             psZ[:, :].rearrange("p (h t) -> p h t", h=4), ACT.Copy).then_inc(at_act, 1)
                if slot == AT_AT["half"]:
                    act.wait_ge(at_pe, AT_PE.after(g, "pv"))
                    if not (isinstance(g, int) and g == 0):
                        act.wait_ge(at_dve, AT_DVE.after(g - 1, "sum"))
                    nc.scalar.activation(o_half[0:LAT, :], psZ[LAT:2 * LAT, T:2 * T], ACT.Copy).then_inc(at_act, 1)
                if slot == AT_AT["tanh"]:
                    act.wait_ge(at_dve, AT_DVE.after(g, "sum"))
                    nc.scalar.activation(th[0:LAT, :], o[0:LAT, :], ACT.Tanh, scale=0.851).then_inc(at_act, 1)

            def experts(p, slot):
                if slot == EX_AT["turn"] + 1:
                    act.wait_ge(ex_pe, EX_PE.after(p, "turn"))
                    for b in range(2):
                        nc.scalar.activation(xa[0:LAT, b * T:b * T + T], psZ[b * LAT:b * LAT + LAT, 0:T],
                                             ACT.Copy).then_inc(ex_act, 1)
                if slot == EX_AT["turnoh"] + 1:
                    act.wait_ge(ex_pe, EX_PE.after(p, "turnoh"))
                    nc.scalar.activation(xa[96:128, :], psZ[0:E, 0:2 * T], ACT.Copy).then_inc(ex_act, 1)
                    nc.scalar.activation(ohT[0:E, :], psZ[0:E, 0:2 * T], ACT.Identity, bias=one[0:E, 0:1],
                                         scale=-1.0).then_inc(ex_act, 1)
                for n, name in enumerate(("hida", "hidb")):
                    if slot == EX_AT[name] + 1:
                        act.wait_ge(ex_pe, EX_PE.after(p, name))
                        nc.scalar.activation(hT[:, 2 * n:2 * n + 2, :].rearrange("p a t -> p (a t)"), psZ[:, :],
                                             ACT.Relu).then_inc(ex_act, 1)
                if slot == EX_AT["out"] + 1:
                    act.wait_ge(ex_pe, EX_PE.after(p, "out"))
                    for b in range(2):
                        nc.scalar.activation(fT[b * LAT:b * LAT + LAT, :], psZ[0:LAT, b * T:b * T + T],
                                             ACT.Relu).then_inc(ex_act, 1)

            def prologue():
                act.wait_ge(loaded_first, FIRST)
                act.wait_ge(ready, READY)
                for s in range(SLOTS):
                    if s == TOK_AT["conv2"]:
                        act.wait_ge(loaded, LOADED)
                    tok(0, s)
                for s in range(SLOTS):
                    norm(0, s)
                    kq(0, 0, s - SECOND)
                    tok(1, s)

            def iteration(i, late=True, tokens=True, ahead=True):
                for s in range(SLOTS):
                    unit(i, s)
                    if late:
                        attend(i - 1, 1, s)
                    kq(i, 1, s)
                    if late:
                        experts(i - 1, s)
                    hand(i, s)
                    if ahead:
                        norm(i + 1, s)
                    attend(i, 0, s - SECOND)
                    if ahead:
                        kq(i + 1, 0, s - SECOND)
                    if tokens:
                        tok(i + 2, s)

            def epilogue():
                for s in range(SLOTS):
                    attend(PAIRS - 1, 1, s)
                    experts(PAIRS - 1, s)

            program(act, prologue, iteration, epilogue)

        @block.vector
        def _(dve):
            def unit(i, slot):
                if shared(slot):
                    return
                b, c, hd = slot // 64, slot // HEADS % CHUNKS, slot % HEADS
                n = D_BEFORE[slot]
                if slot % 64 == 0 and not (isinstance(i, int) and i == 0):
                    dve.wait_ge(at_act, AT_ACT.after(2 * i + b - 2, "exp7"))
                dve.wait_ge(d_made, D_PAIR * i + n + 1)
                nc.vector.tensor_reduce(S[:, b, hd, SB * c:SB * c + SB],
                                        psU[:, slot % PLACES].rearrange("p a s w -> p s a w"), AX.XY, ALU.add,
                                        apply_absolute_value=True).then_inc(d_done, 1)

            def stats(x, name, sm, after):
                for b in range(2):
                    nc.vector.bn_stats(st[name][:, b, :], x[:, b, :]).then_inc(sm, 1)
                dve.wait_ge(sm, after("stat1"))
                nc.vector.memset(spare[:, :], 0.0).then_inc(sm, 1)
                for b in range(2):
                    nc.vector.bn_aggr(mv[name][:, b, :], st[name][:, b, :]).then_inc(sm, 1)
                dve.wait_ge(sm, after("aggr1"))
                nc.vector.tensor_scalar_add(ve[name][:, :], mv[name][:, :, 1], EPS).then_inc(sm, 1)

            def affine(x, name, g, bb, dst, n, p):
                for b in range(2):
                    nc.vector.scalar_tensor_tensor(lt[:, b, 0:n], x[:, b, :], mv[name][:, b, 0:1], g[:, :],
                                                   ALU.subtract, ALU.mult).then_inc(tok_dve, 1)
                dve.wait_ge(tok_pool, TOK_POOL.after(p, "rstd" + name))
                for b in range(2):
                    dve.wait_ge(tok_dve, TOK_DVE.after(p, f"gain{name}{b}"))
                    nc.vector.scalar_tensor_tensor(dst[:, b, 2:2 + J, :].rearrange("p j w -> p (j w)"),
                                                   lt[:, b, 0:n], rstd[name][:, b:b + 1], bb[:, :],
                                                   ALU.mult, ALU.add).then_inc(tok_dve, 1)

            def tok(p, slot):
                def after(name):
                    return lambda s: TOK_DVE.after(p, s[:-1] + name + s[-1])
                if slot == TOK_AT["a"]:
                    dve.wait_ge(x_in, 16 * (p + 1))
                    if not (isinstance(p, int) and p == 0):
                        dve.wait_ge(tok_dve, TOK_DVE.after(p - 1, "h"))
                    stats(xin, "a", tok_dve, after("a"))
                if slot == TOK_AT["a"] + TOK_AT["gap"]:
                    affine(xin, "a", ln0g, ln0b, c1in, 3 * J, p)
                if slot == TOK_AT["b"]:
                    dve.wait_ge(tok_act, TOK_ACT.after(p, "relu1"))
                    stats(y1, "b", tok_dve, after("b"))
                if slot == TOK_AT["b"] + TOK_AT["gap"]:
                    affine(y1, "b", ln0g, ln0b, c2in, 3 * J, p)
                if slot == TOK_AT["c"]:
                    dve.wait_ge(tok_act, TOK_ACT.after(p, "relu2"))
                    stats(y2, "c", tok_dve, after("c"))
                if slot == TOK_AT["c"] + TOK_AT["gap"]:
                    affine(y2, "c", ln1g, ln1b, c3in, 2 * J, p)
                if slot == TOK_AT["d"]:
                    dve.wait_ge(tok_act, TOK_ACT.after(p, "relu3b"))
                    stats(res, "d", tok_dve, after("d"))
                if slot == TOK_AT["d"] + TOK_AT["gap"]:
                    dve.wait_ge(tok_pool, TOK_POOL.after(p, "rstdd"))
                    for b in range(2):
                        nc.vector.tensor_scalar(resn[:, b, :], res[:, b, :], mv["d"][:, b, 0:1], rstd["d"][:, b:b + 1],
                                                ALU.subtract, ALU.mult).then_inc(tok_dve, 1)
                if slot == TOK_AT["out"] + 1:
                    dve.wait_ge(tok_pe, TOK_PE.after(p, "out"))
                    if not (isinstance(p, int) and p == 0):
                        dve.wait_ge(norm_pool, NORM_POOL.after(p - 1, "hx"))
                    nc.vector.tensor_tensor(h[:, :, :], psC[:, 0:2 * LAT].rearrange("p (b w) -> p b w", b=2),
                                            bout[:, :, :], ALU.add).then_inc(tok_dve, 1)

            def norm(p, slot):
                if slot == NORM_AT["stat"]:
                    dve.wait_ge(tok_dve, TOK_DVE.after(p, "h"))
                    stats(h, "n", norm_dve, lambda s: NORM_DVE.after(p, s))
                if slot == NORM_AT["x"]:
                    dve.wait_ge(norm_pool, NORM_POOL.after(p, "rstd"))
                    if not (isinstance(p, int) and p == 0):
                        dve.wait_ge(keys_pool, K_POOL.after(2 * p - 1, "k"))
                    for b in range(2):
                        nc.vector.tensor_scalar(x1[:, b, :], h[:, b, :], mv["n"][:, b, 0:1], rstd["n"][:, b:b + 1],
                                                ALU.subtract, ALU.mult).then_inc(norm_dve, 1)

            def kq(p, b, slot):
                g = 2 * p + b
                if slot == KQ_AT["qrest1"]:
                    dve.wait_ge(queries_act, Q_ACT.after(g, "qpart1"))
                    if not (isinstance(g, int) and g == 0):
                        dve.wait_ge(queries_pool, Q_POOL.after(g - 1, "qpart3"))
                    nc.vector.tensor_tensor(qrest[:, :], psZ[:, :], qparts[:, b, 0, :],
                                            ALU.subtract).then_inc(queries_dve, 1)

            def attend(p, b, slot):
                g = 2 * p + b
                if slot == AT_AT["den"]:
                    dve.wait_ge(at_act, AT_ACT.after(g, "exp7"))
                    nc.vector.tensor_scalar_add(den1[:, :], den[:, :], 1.0).then_inc(at_dve, 1)
                    dve.wait_ge(at_dve, AT_DVE.after(g, "den"))
                    nc.vector.reciprocal(rden[:, :], den1[:, :]).then_inc(at_dve, 1)
                if slot == AT_AT["sum"]:
                    dve.wait_ge(at_act, AT_ACT.after(g, "half"))
                    if not (isinstance(g, int) and g == 0):
                        dve.wait_ge(at_dve, AT_DVE.after(g - 1, "gate"))
                    nc.vector.tensor_tensor(o[0:LAT, :], psZ[0:LAT, 0:T], o_half[0:LAT, :], ALU.add)\
                        .then_inc(at_dve, 1)
                if slot == AT_AT["gate"]:
                    dve.wait_ge(at_act, AT_ACT.after(g, "tanh"))
                    nc.vector.scalar_tensor_tensor(gT[0:LAT, b, :], th[0:LAT, :], 1.0, o[0:LAT, :],
                                                   ALU.add, ALU.mult).then_inc(at_dve, 1)

            def experts(p, slot):
                def done(name):
                    return EX_DVE.after(p, name)
                zr = psZ[:, 0:2 * E].rearrange("p (b e) -> p b e", b=2)
                zl = psZ[:, 0:2 * LAT].rearrange("p (b w) -> p b w", b=2)
                if slot == EX_AT["h2"]:
                    dve.wait_ge(ex_pe, EX_PE.after(p, "fan"))
                    dve.wait_ge(hand_act, HAND_ACT.after(p, "hx"))
                    nc.vector.scalar_tensor_tensor(h2[:, :, :], zl, 0.5, hx_late[:, :, :],
                                                   ALU.mult, ALU.add).then_inc(ex_dve, 1)
                    dve.wait_ge(ex_dve, done("h2"))
                    stats(h2, "e", ex_dve, done)
                if slot == EX_AT["x"]:
                    dve.wait_ge(ex_pool, EX_POOL.after(p, "rstd"))
                    for b in range(2):
                        nc.vector.tensor_scalar(x2[:, b, :], h2[:, b, :], mv["e"][:, b, 0:1], rstd["e"][:, b:b + 1],
                                                ALU.subtract, ALU.mult).then_inc(ex_dve, 1)
                if slot == EX_AT["pick"]:
                    dve.wait_ge(ex_pe, EX_PE.after(p, "route"))
                    nc.vector.tensor_reduce(top[:, :], zr, AX.X, ALU.max).then_inc(ex_dve, 1)
                    dve.wait_ge(ex_dve, done("max"))
                    nc.vector.tensor_tensor(eq[:, :, :], zr, top[:, :].unsqueeze(2).broadcast_to([T, 2, E]),
                                            ALU.is_ge).then_inc(ex_dve, 1)
                    dve.wait_ge(ex_dve, done("eq"))
                    nc.vector.tensor_tensor(rev[:, :, :], eq[:, :, :], rank[:, :, :], ALU.mult).then_inc(ex_dve, 1)
                    dve.wait_ge(ex_dve, done("rev"))
                    nc.vector.tensor_reduce(top2[:, :], rev[:, :, :], AX.X, ALU.max).then_inc(ex_dve, 1)
                    dve.wait_ge(ex_dve, done("max2"))
                    nc.vector.tensor_tensor(noh[:, :, :], rev[:, :, :], top2[:, :].unsqueeze(2).broadcast_to([T, 2, E]),
                                            ALU.is_lt).then_inc(ex_dve, 1)
                if slot == EX_AT["back"] + 1:
                    dve.wait_ge(ex_pe, EX_PE.after(p, "back"))
                    if not (isinstance(p, int) and p == 0):
                        dve.wait_ge(stored, 16 * p)
                    nc.vector.tensor_tensor(result[:, :, :], zl, h2[:, :, :], ALU.add).then_inc(ex_dve, 1)

            def prologue():
                for t in (c1in, c2in, c3in, xa, ohT):
                    nc.vector.memset(t[:], 0.0).then_inc(ready, 1)
                nc.vector.memset(be2[32:64, :], 0.0).then_inc(ready, 1)
                nc.vector.memset(be2[64:128, :], 0.0).then_inc(ready, 1)
                nc.vector.memset(we1[64:96, :], 0.0).then_inc(zeroed, 1)
                for t in (x1T, x1T_late):
                    nc.vector.memset(t[64:65, :], 1.0).then_inc(ready, 1)
                nc.vector.memset(gT[64:65, :, :], 2.0).then_inc(ready, 1)
                nc.vector.memset(kT[96:99], -1.0).then_inc(ready, 1)
                nc.vector.memset(half[:, :], -0.5).then_inc(ready, 1)
                nc.vector.memset(one[:, :], 1.0).then_inc(ready, 1)
                dve.wait_ge(ready, 13)
                nc.vector.memset(xa[64:65, :], 1.0).then_inc(ready, 1)
                dve.wait_ge(loaded_first, FIRST)
                nc.vector.tensor_copy(ident_b[:, :], ident[:, :]).then_inc(ready, 1)

                def fill(part):
                    rows = slice(32 * part, 32 * part + 32)
                    nc.vector.tensor_copy(
                        flat[rows].rearrange("p r s (n w) -> p (r s n) w", w=32),
                        ident_b[rows, rows].unsqueeze(1).broadcast_to([32, RING * SB * HW // 32, 32])) \
                        .then_inc(filled, 1)

                dve.wait_ge(ready, READY)
                for s in range(SLOTS):
                    tok(0, s)
                    if s == TOK_AT["conv1"]:
                        fill(0)
                        dve.wait_ge(loaded, LOADED)
                    if s == TOK_AT["conv3"]:
                        fill(1)
                for s in range(SLOTS):
                    norm(0, s)
                    kq(0, 0, s - SECOND)
                    tok(1, s)
                    if s == TOK_AT["conv1"]:
                        fill(2)

            def iteration(i, late=True, tokens=True, ahead=True):
                for s in range(SLOTS):
                    unit(i, s)
                    if late:
                        attend(i - 1, 1, s)
                    kq(i, 1, s)
                    if late:
                        experts(i - 1, s)
                    if ahead:
                        norm(i + 1, s)
                    attend(i, 0, s - SECOND)
                    if ahead:
                        kq(i + 1, 0, s - SECOND)
                    if tokens:
                        tok(i + 2, s)

            def epilogue():
                for s in range(SLOTS):
                    attend(PAIRS - 1, 1, s)
                    experts(PAIRS - 1, s)

            program(dve, prologue, iteration, epilogue)

        @block.gpsimd
        def _(pool):
            def unit(i, slot):
                if not shared(slot) or A_BEFORE[slot] % 2 == 0:
                    return
                b, c, hd = slot // 64, slot // HEADS % CHUNKS, slot % HEADS
                n = A_BEFORE[slot]
                heads = SHARED[slot // HEADS]
                first = heads[heads.index(hd) - 1]
                buf = n // 2 % GROUPS
                base = LEVELS * (TREES * i + n // 2)
                pool.wait_ge(a_abs, A_PAIR * i + n + 1)
                t = absd[:, buf]
                lo, hi = (t[:, :, m].rearrange("p u s w -> p u (s w)") for m in range(2))
                nc.gpsimd.tensor_tensor(lo, lo, hi, ALU.add).then_inc(a_tree, 1)
                w = 32
                for level in range(1, LEVELS):
                    w //= 2
                    lo, hi = t[:, :, 0, :, 0:w], t[:, :, 0, :, w:2 * w]
                    dst = lo
                    if level == LEVELS - 1:
                        dst = S[:, b, first:hd + 1:hd - first, SB * c:SB * c + SB].unsqueeze(3)
                        if slot % 64 < 8 and not (isinstance(i, int) and i == 0):
                            pool.wait_ge(at_act, AT_ACT.after(2 * i + b - 2, "exp7"))
                    pool.wait_ge(a_tree, base + level)
                    nc.gpsimd.tensor_tensor(dst, lo, hi, ALU.add).then_inc(a_tree, 1)

            def root(name, dve_sem, value, pool_sem):
                pool.wait_ge(dve_sem, value)
                nc.gpsimd.tensor_tensor(rstd[name][:, :], ve[name][:, :], half[:, :], ALU.pow).then_inc(pool_sem, 1)

            def tok(p, slot):
                for name in "abcd":
                    if slot == TOK_AT[name] + TOK_AT["root"]:
                        root(name, tok_dve, TOK_DVE.after(p, "eps" + name), tok_pool)

            def norm(p, slot):
                if slot == NORM_AT["rstd"]:
                    root("n", norm_dve, NORM_DVE.after(p, "eps"), norm_pool)
                if slot == NORM_AT["hx"]:
                    pool.wait_ge(norm_dve, NORM_DVE.after(p, "x1"))
                    if not (isinstance(p, int) and p == 0):
                        pool.wait_ge(hand_act, HAND_ACT.after(p - 1, "hx"))
                    nc.gpsimd.tensor_tensor(hx[:, :, :], h[:, :, :], x1[:, :, :], ALU.add).then_inc(norm_pool, 1)

            def kq(p, b, slot):
                g = 2 * p + b
                if slot == KQ_AT["k"]:
                    pool.wait_ge(norm_dve, NORM_DVE.after(p, "x1"))
                    if not (isinstance(g, int) and g == 0):
                        pool.wait_ge(keys_pool, K_POOL.after(g - 1, "part3"))
                    nc.gpsimd.tensor_tensor(k[:, :, :, :].rearrange("p h a w -> p h (a w)"),
                                            x1[:, b, :].unsqueeze(1).broadcast_to([T, HEADS, LAT]),
                                            wk[:, :, :], ALU.mult).then_inc(keys_pool, 1)
                if slot == KQ_AT["rest1"]:
                    pool.wait_ge(keys_act, K_ACT.after(g, "part1"))
                    nc.gpsimd.tensor_tensor(k[:, :, :, :], k[:, :, :, :], kparts[:, :, :, 0, :],
                                            ALU.subtract).then_inc(keys_pool, 1)
                if slot == KQ_AT["part3"]:
                    pool.wait_ge(keys_act, K_ACT.after(g, "part2"))
                    nc.gpsimd.tensor_tensor(kparts[:, :, :, 2, :], k[:, :, :, :], kparts[:, :, :, 1, :],
                                            ALU.subtract).then_inc(keys_pool, 1)
                if slot == KQ_AT["qpart3"]:
                    pool.wait_ge(queries_act, Q_ACT.after(g, "qpart2"))
                    nc.gpsimd.tensor_tensor(qparts[:, b, 2, :], qrest[:, :], qparts[:, b, 1, :],
                                            ALU.subtract).then_inc(queries_pool, 1)

            def experts(p, slot):
                if slot == EX_AT["rstd"]:
                    root("e", ex_dve, EX_DVE.after(p, "eps"), ex_pool)

            def prologue():
                pool.wait_ge(ready, READY)
                for s in range(SLOTS):
                    if s == TOK_AT["conv2"]:
                        pool.wait_ge(loaded, LOADED)
                    tok(0, s)
                for s in range(SLOTS):
                    norm(0, s)
                    kq(0, 0, s - SECOND)
                    tok(1, s)

            def iteration(i, late=True, tokens=True, ahead=True):
                for s in range(SLOTS):
                    unit(i, s)
                    kq(i, 1, s)
                    if late:
                        experts(i - 1, s)
                    if ahead:
                        norm(i + 1, s)
                    if ahead:
                        kq(i + 1, 0, s - SECOND)
                    if tokens:
                        tok(i + 2, s)

            def epilogue():
                for s in range(SLOTS):
                    experts(PAIRS - 1, s)

            program(pool, prologue, iteration, epilogue)


def lay_out(x, L0_tok_ln0_g, L0_tok_ln0_b, L0_tok_ln1_g, L0_tok_ln1_b, L0_tok_conv1_w, L0_tok_conv1_b,
            L0_tok_conv2_w, L0_tok_conv2_b, L0_tok_conv3_w, L0_tok_conv3_b, L0_tok_out_w, L0_tok_out_b,
            L0_attn_wqv_w, L0_attn_wqv_b, L0_attn_wk, L0_attn_fanin_w, L0_attn_fanin_b, L0_ffn_router_w,
            L0_ffn_router_b, L0_ffn_W1, L0_ffn_b1, L0_ffn_W2, L0_ffn_b2):
    import numpy as np

    def rows(v, *shape):
        return np.broadcast_to(np.reshape(v, (1,) + shape), (T,) + shape)

    def taps(w):
        w = np.transpose(w, (1, 2, 3, 0))
        return w.reshape(w.shape[0], -1, w.shape[3])

    def with_bias(w, b):
        return np.concatenate([w, np.reshape(b, (1, -1))], axis=0)

    shut = np.zeros((E, E, HID), np.float32)
    shut[np.arange(E), np.arange(E), :] = NOT_CHOSEN
    d = {
        "x": np.reshape(x, (x.shape[0], T, 3 * J)),
        "ident": np.eye(T, dtype=np.float32),
        "ln0g": rows(L0_tok_ln0_g, 3 * J), "ln0b": rows(L0_tok_ln0_b, 3 * J),
        "ln1g": rows(L0_tok_ln1_g, 2 * J), "ln1b": rows(L0_tok_ln1_b, 2 * J),
        "ln1g_col": np.reshape(L0_tok_ln1_g, (T, 1)), "ln1b_col": np.reshape(L0_tok_ln1_b, (T, 1)),
        "w1": taps(L0_tok_conv1_w), "w2": taps(L0_tok_conv2_w), "w3": taps(L0_tok_conv3_w),
        "b1": np.reshape(L0_tok_conv1_b, (T, 1)), "b2": np.reshape(L0_tok_conv2_b, (T, 1)),
        "b3": np.transpose(np.reshape(L0_tok_conv3_b, (2, T))),
        "wout": L0_tok_out_w,
        "bout": np.broadcast_to(np.reshape(L0_tok_out_b, (1, 1, LAT)), (T, 2, LAT)),
        "wqv": with_bias(np.transpose(L0_attn_wqv_w), L0_attn_wqv_b),
        "wk": rows(L0_attn_wk, HEADS, LAT),
        "wfan": with_bias(np.transpose(L0_attn_fanin_w), L0_attn_fanin_b),
        "wroute": with_bias(np.transpose(L0_ffn_router_w), L0_ffn_router_b),
        "we1": with_bias(np.reshape(np.transpose(L0_ffn_W1, (1, 0, 2)), (LAT, E * HID)), L0_ffn_b1),
        "shut": np.reshape(shut, (E, E * HID)),
        "we2": np.transpose(np.reshape(L0_ffn_W2, (4, T, LAT)), (1, 0, 2)),
        "be2": L0_ffn_b2,
        "rank": np.broadcast_to((E - np.arange(E, dtype=np.float32)).reshape(1, 1, E), (T, 2, E)),
    }
    return {name: np.ascontiguousarray(v) for name, v in d.items()}


def kernel(**inputs):
    import numpy as np
    from concourse import bacc, mybir as mb
    from concourse.bass_utils import run_bass_kernel_spmd

    arrays = lay_out(**{name: np.asarray(v) for name, v in inputs.items()})
    nc = bacc.Bacc("TRN2", target_bir_lowering=False, num_devices=1)
    aps = {name: nc.dram_tensor("in_" + name, v.shape, mb.dt.from_np(v.dtype), kind="ExternalInput").ap()
           for name, v in arrays.items()}
    out = nc.dram_tensor("out_h", (arrays["x"].shape[0], T, LAT), F32, kind="ExternalOutput").ap()
    vit_tower(nc, aps, out)
    r = run_bass_kernel_spmd(nc, [{"in_" + name: v for name, v in arrays.items()}], core_ids=[0])
    return r.results[0]["out_h"]
```
